# Optimizing a Trainium2 kernel written in Bass

```python
import numpy as np
import jax
import jax.numpy as jnp

def _softmax(x, axis=-1):
    return jax.nn.softmax(x, axis=axis)

def _gelu(x):
    return jax.nn.gelu(x, approximate=True)

def _silu(x):
    return jax.nn.silu(x)

def _sigmoid(x):
    return jax.nn.sigmoid(x)

def _layernorm(x, axis=-1, eps=1e-05):
    m = jnp.mean(x, axis=axis, keepdims=True)
    v = jnp.var(x, axis=axis, keepdims=True)
    return (x - m) / jnp.sqrt(v + eps)

def _scatter_add(tgt, idx, src, axis=0):
    return tgt.at[idx].add(src)

def _segment_sum(src, seg, n):
    return jax.ops.segment_sum(src, seg, n)
kernel_name = 'mk_macaron_d1_jaxref_r8_69a1c3'

def setup_inputs(seed: int=0):
    np.random.seed(seed)
    _w = jnp.asarray

    def _L0_attn_setup():
        import jax, jax.numpy as jnp
        import numpy as np
        D_MODEL = 128
        NUM_HEADS = 16
        DEPTH = D_MODEL // NUM_HEADS
        EPS_LN = 0.001
        EPS_QK = 1e-06

        def _split_heads(t):
            B, L, _ = t.shape
            return t.reshape(B, L, NUM_HEADS, DEPTH).transpose(0, 2, 1, 3)

        def _forward(x, Wq, bq, Wk, bk, Wv, bv, Wq2, bq2, Wk2, bk2, Wv2, bv2, Wo, bo, gamma, beta):
            B, L, _ = x.shape
            q = x @ Wq + bq
            k = x @ Wk + bk
            v = x @ Wv + bv
            q = _split_heads(q @ Wq2 + bq2)
            k = _split_heads(k @ Wk2 + bk2)
            v = _split_heads(v @ Wv2 + bv2)
            q = jax.nn.elu(q) + 1.0
            k = jax.nn.elu(k) + 1.0
            S = jnp.einsum('bhld,bhle->bhde', k, q)
            out = jnp.einsum('bhmd,bhde->bhme', v, S)
            qks = jnp.einsum('bhld,bhld->bhl', q, k) + EPS_QK
            out = out / qks[..., None]
            out = out.transpose(0, 2, 1, 3).reshape(B, L, D_MODEL)
            out = out @ Wo + bo
            y = x + out
            mu = jnp.mean(y, axis=-1, keepdims=True)
            var = jnp.var(y, axis=-1, keepdims=True)
            return gamma * (y - mu) * jax.lax.rsqrt(var + EPS_LN) + beta
        key = jax.random.key(seed)
        ks = jax.random.split(key, 16)
        s = 1.0 / np.sqrt(D_MODEL)

        def W(k):
            return jax.random.normal(k, (D_MODEL, D_MODEL), jnp.float32) * s

        def b(k):
            return jnp.zeros((D_MODEL,), jnp.float32)
        return {'x': jax.random.normal(ks[0], (4, 512, D_MODEL), jnp.float32), 'Wq': W(ks[1]), 'bq': b(ks[1]), 'Wk': W(ks[2]), 'bk': b(ks[2]), 'Wv': W(ks[3]), 'bv': b(ks[3]), 'Wq2': W(ks[4]), 'bq2': b(ks[4]), 'Wk2': W(ks[5]), 'bk2': b(ks[5]), 'Wv2': W(ks[6]), 'bv2': b(ks[6]), 'Wo': W(ks[7]), 'bo': b(ks[7]), 'gamma': jnp.ones((D_MODEL,), jnp.float32), 'beta': jnp.zeros((D_MODEL,), jnp.float32)}
    _L0_attn_in = _L0_attn_setup()

    def _L0_ffn_setup():
        import jax, jax.numpy as jnp
        import numpy as np
        TEMPERATURE = 1.0
        TOPK = 2
        key = jax.random.key(seed)
        ks = jax.random.split(key, 6)
        S, B, H, F, E = (256, 4, 128, 512, 8)
        x = jax.random.normal(ks[0], (S, B, H), dtype=jnp.float32)
        gate_w = jax.random.normal(ks[1], (E, H), dtype=jnp.float32) * (1.0 / np.sqrt(H))
        w1 = jax.random.normal(ks[2], (E, H, F), dtype=jnp.float32) * (1.0 / np.sqrt(H))
        b1 = jnp.zeros((E, F), dtype=jnp.float32)
        w2 = jax.random.normal(ks[3], (E, F, H), dtype=jnp.float32) * (1.0 / np.sqrt(F))
        b2 = jnp.zeros((E, H), dtype=jnp.float32)
        return {'x': x, 'gate_w': gate_w, 'w1': w1, 'b1': b1, 'w2': w2, 'b2': b2}
    _L0_ffn_in = _L0_ffn_setup()
    _d = {'L0_attn_x': _L0_attn_in['x'], 'L0_attn_Wq': _L0_attn_in['Wq'], 'L0_attn_bq': _L0_attn_in['bq'], 'L0_attn_Wk': _L0_attn_in['Wk'], 'L0_attn_bk': _L0_attn_in['bk'], 'L0_attn_Wv': _L0_attn_in['Wv'], 'L0_attn_bv': _L0_attn_in['bv'], 'L0_attn_Wq2': _L0_attn_in['Wq2'], 'L0_attn_bq2': _L0_attn_in['bq2'], 'L0_attn_Wk2': _L0_attn_in['Wk2'], 'L0_attn_bk2': _L0_attn_in['bk2'], 'L0_attn_Wv2': _L0_attn_in['Wv2'], 'L0_attn_bv2': _L0_attn_in['bv2'], 'L0_attn_Wo': _L0_attn_in['Wo'], 'L0_attn_bo': _L0_attn_in['bo'], 'L0_attn_gamma': _L0_attn_in['gamma'], 'L0_attn_beta': _L0_attn_in['beta'], 'L0_ffn_gate_w': _L0_ffn_in['gate_w'], 'L0_ffn_w1': _L0_ffn_in['w1'], 'L0_ffn_b1': _L0_ffn_in['b1'], 'L0_ffn_w2': _L0_ffn_in['w2'], 'L0_ffn_b2': _L0_ffn_in['b2']}
    _x0 = _d['L0_attn_x']
    _d['L0_attn_x'] = jax.random.normal(jax.random.fold_in(jax.random.key(seed), 1), (4, 1024, 128), dtype=_x0.dtype)
    del _x0
    return _d

def reference(L0_attn_x, L0_attn_Wq, L0_attn_bq, L0_attn_Wk, L0_attn_bk, L0_attn_Wv, L0_attn_bv, L0_attn_Wq2, L0_attn_bq2, L0_attn_Wk2, L0_attn_bk2, L0_attn_Wv2, L0_attn_bv2, L0_attn_Wo, L0_attn_bo, L0_attn_gamma, L0_attn_beta, L0_ffn_gate_w, L0_ffn_w1, L0_ffn_b1, L0_ffn_w2, L0_ffn_b2):

    def _L0_attn_ref(x, Wq, bq, Wk, bk, Wv, bv, Wq2, bq2, Wk2, bk2, Wv2, bv2, Wo, bo, gamma, beta):
        import jax, jax.numpy as jnp
        import numpy as np
        D_MODEL = 128
        NUM_HEADS = 16
        DEPTH = D_MODEL // NUM_HEADS
        EPS_LN = 0.001
        EPS_QK = 1e-06

        def _split_heads(t):
            B, L, _ = t.shape
            return t.reshape(B, L, NUM_HEADS, DEPTH).transpose(0, 2, 1, 3)

        def _forward(x, Wq, bq, Wk, bk, Wv, bv, Wq2, bq2, Wk2, bk2, Wv2, bv2, Wo, bo, gamma, beta):
            B, L, _ = x.shape
            q = x @ Wq + bq
            k = x @ Wk + bk
            v = x @ Wv + bv
            q = _split_heads(q @ Wq2 + bq2)
            k = _split_heads(k @ Wk2 + bk2)
            v = _split_heads(v @ Wv2 + bv2)
            q = jax.nn.elu(q) + 1.0
            k = jax.nn.elu(k) + 1.0
            S = jnp.einsum('bhld,bhle->bhde', k, q)
            out = jnp.einsum('bhmd,bhde->bhme', v, S)
            qks = jnp.einsum('bhld,bhld->bhl', q, k) + EPS_QK
            out = out / qks[..., None]
            out = out.transpose(0, 2, 1, 3).reshape(B, L, D_MODEL)
            out = out @ Wo + bo
            y = x + out
            mu = jnp.mean(y, axis=-1, keepdims=True)
            var = jnp.var(y, axis=-1, keepdims=True)
            return gamma * (y - mu) * jax.lax.rsqrt(var + EPS_LN) + beta
        return _forward(x, Wq, bq, Wk, bk, Wv, bv, Wq2, bq2, Wk2, bk2, Wv2, bv2, Wo, bo, gamma, beta)

    def _L0_ffn_ref(x, gate_w, w1, b1, w2, b2):
        import jax, jax.numpy as jnp
        import numpy as np
        TEMPERATURE = 1.0
        TOPK = 2
        s, b, h = x.shape
        x_flat = x.reshape(s * b, h)
        logits = x_flat @ gate_w.T
        probs = jax.nn.softmax(logits / TEMPERATURE, axis=-1)
        topk_probs, topk_idx = jax.lax.top_k(probs, TOPK)
        hidden = jax.nn.relu(jnp.einsum('th,ehf->tef', x_flat, w1) + b1[None])
        all_out = jnp.einsum('tef,efh->teh', hidden, w2) + b2[None]
        gathered = jnp.take_along_axis(all_out, topk_idx[:, :, None], axis=1)
        y_flat = jnp.sum(gathered * topk_probs[:, :, None], axis=1)
        return y_flat.reshape(s, b, h)
    x = L0_attn_x
    x = x + 0.5 * _L0_ffn_ref(_layernorm(x, axis=-1), L0_ffn_gate_w, L0_ffn_w1, L0_ffn_b1, L0_ffn_w2, L0_ffn_b2)
    x = x + _L0_attn_ref(_layernorm(x, axis=-1), L0_attn_Wq, L0_attn_bq, L0_attn_Wk, L0_attn_bk, L0_attn_Wv, L0_attn_bv, L0_attn_Wq2, L0_attn_bq2, L0_attn_Wk2, L0_attn_bk2, L0_attn_Wv2, L0_attn_bv2, L0_attn_Wo, L0_attn_bo, L0_attn_gamma, L0_attn_beta)
    x = x + 0.5 * _L0_ffn_ref(_layernorm(x, axis=-1), L0_ffn_gate_w, L0_ffn_w1, L0_ffn_b1, L0_ffn_w2, L0_ffn_b2)
    return x

_drawn_inputs = setup_inputs


def setup_inputs(seed=0):
    import zlib

    import numpy as np

    out = dict(_drawn_inputs(seed))
    spreads = {'L0_attn_bq': (0.0, 0.1),
     'L0_attn_bk': (0.0, 0.1),
     'L0_attn_bv': (0.0, 0.1),
     'L0_attn_bq2': (0.0, 0.1),
     'L0_attn_bk2': (0.0, 0.1),
     'L0_attn_bv2': (0.0, 0.1),
     'L0_attn_bo': (0.0, 0.8),
     'L0_attn_gamma': (1.0, 0.2),
     'L0_attn_beta': (0.0, 0.1),
     'L0_ffn_b1': (0.0, 0.341),
     'L0_ffn_b2': (0.0, 0.1)}
    factors = {}
    for name, (base, spread) in spreads.items():
        noise = np.random.default_rng([zlib.crc32(name.encode()), seed]).standard_normal(out[name].shape)
        drawn = base * np.exp(spread * noise) if base else spread * noise
        out[name] = jnp.asarray(drawn.astype(out[name].dtype))
    for name, factor in factors.items():
        out[name] = (out[name] * factor).astype(out[name].dtype)
    return out
```

```python
from contextlib import ExitStack

import concourse.bass as bass
from concourse import mybir

P = 128
B, L, D = 4, 1024, 128
E, F, TOPK = 8, 512, 2
H, DH = 16, 8
J = L // P
NC = TOPK * J
FC = F // P
NT = (L * TOPK - E) // P + E
SLOTS = NT * P
NTP = NT + 1
XS = 16.0
EPS_FFN, EPS_ATTN_OUT, EPS_QK = 1e-5, 1e-3, 1e-6

ALU = mybir.AluOpType
ACT = mybir.ActivationFunctionType
AX = mybir.AxisListType.X
F32, F16, I32, U32 = mybir.dt.float32, mybir.dt.float16, mybir.dt.int32, mybir.dt.uint32
RMAX = bass.bass_isa.ReduceOp.max



def macaron(nc, A_x, Wq, bq, Wk, bk, Wv, bv, Wq2, bq2, Wk2, bk2, Wv2, bv2, Wo, bo, gamma, beta,
            gate_w, w1, b1, w2, b2, out):
    with ExitStack() as ctx:
        def sb(name, shape, dt=F32):
            return ctx.enter_context(nc.sbuf_tensor(name, shape, dt))

        def ps(name, shape, dt=F32):
            return ctx.enter_context(nc.psum_tensor(name, shape, dt))

        def sem(name):
            return ctx.enter_context(nc.semaphore(name))

        s_x_in = sem("x_in")
        s_w1_in = sem("w1_in")
        s_w2_in = sem("w2_in")
        s_b1_in = sem("b1_in")
        s_b2_in = sem("b2_in")
        s_gate_in = sem("gate_in")
        s_wqkv_in = sem("wqkv_in")
        s_wqkv2_in = sem("wqkv2_in")
        s_wo_in = sem("wo_in")
        s_bcol_in = sem("bcol_in")
        s_brow_in = sem("brow_in")
        s_zero_set = sem("zero_set")
        s_xs_zeroed = sem("xs_zeroed")
        s_consts = sem("consts")
        s_dve_order = sem("dve_order")
        s_absmax = sem("absmax")
        s_absmax_all = sem("absmax_all")
        s_scales = sem("scales")
        s_w1_hi = sem("w1_hi")
        s_w2_hi = sem("w2_hi")
        s_w1_lo = sem("w1_lo")
        s_w2_lo = sem("w2_lo")
        s_b1_hi = sem("b1_hi")
        s_b1_lo = sem("b1_lo")
        s_sel16 = sem("sel16")
        s_b2_zero = sem("b2_zero")
        s_gate_ps = sem("gate_ps")
        s_gate_sb = sem("gate_sb")
        s_wT_ps = sem("wT_ps")
        s_wT_sb = sem("wT_sb")
        s_wf_ps = sem("wf_ps")
        s_wf_sb = sem("wf_sb")
        s_bf_ps = sem("bf_ps")
        s_bf_sb = sem("bf_sb")
        s_ln_stats = sem("ln_stats")
        s_xn = sem("xn")
        s_xhi = sem("xhi")
        s_xs_rows = sem("xs_rows")
        s_xnT_ps = sem("xnT_ps")
        s_xnT_sb = sem("xnT_sb")
        s_logits = sem("logits")
        s_zs = sem("zs")
        s_ez = sem("ez")
        s_e2 = sem("e2")
        s_z2 = sem("z2")
        s_tile_counts = sem("tile_counts")
        s_prefix = sem("prefix")
        s_eids = sem("eids")
        s_gates = sem("gates")
        s_gT_ps = sem("gT_ps")
        s_gT_sb = sem("gT_sb")
        s_b2_ps = sem("b2_ps")
        s_b2_added = sem("b2_added")
        s_pos = sem("pos")
        s_xT_ps = sem("xT_ps")
        s_xT_sb = sem("xT_sb")
        s_h_ps = sem("h_ps")
        s_h_hi = sem("h_hi")
        s_h_lo = sem("h_lo")
        s_y_ps = sem("y_ps")
        s_y_sb = sem("y_sb")
        s_y_stored = sem("y_stored")
        s_gathered = sem("gathered")
        s_comb = sem("comb")
        s_xa = sem("xa")
        s_xaT_ps = sem("xaT_ps")
        s_xaT_sb = sem("xaT_sb")
        s_v_ps = sem("v_ps")
        s_v_sb = sem("v_sb")
        s_q_ps = sem("q_ps")
        s_k_ps = sem("k_ps")
        s_zq = sem("zq")
        s_zk = sem("zk")
        s_eq = sem("eq")
        s_ek = sem("ek")
        s_fq = sem("fq")
        s_fk = sem("fk")
        s_s_ps = sem("s_ps")
        s_s_sb = sem("s_sb")
        s_o_ps = sem("o_ps")
        s_o_sb = sem("o_sb")
        s_oT_ps = sem("oT_ps")
        s_oT_sb = sem("oT_sb")
        s_wo_ps = sem("wo_ps")
        s_yn = sem("yn")
        s_x2 = sem("x2")
        s_out_stored = sem("out_stored")

        scattered = [sem(f"scattered{b}") for b in range(B)]
        slots_in = [[sem(f"slots_in{i}{k}") for k in "abc"] for i in range(2)]

        xs_dram = [nc.dram_tensor(f"xs_dram{b}", [SLOTS, 2 * D], F16).ap() for b in range(B)]
        y_dram = [nc.dram_tensor(f"y_dram{b}", [SLOTS, D], F32).ap() for b in range(B)]

        x = sb("x", [P, B * J, D])
        w1s = sb("w1s", [P, E * 2 * F], F16)
        w2s = sb("w2s", [P, E * 2 * F], F16)
        wraw = sb("wraw", [P, E * F])
        wraw2 = sb("wraw2", [P, E * F])
        b1raw = sb("b1raw", [40, F])
        b1s = sb("b1s", [P, F], F16)
        b1h = sb("b1h", [40, F], F16)
        sel = sb("sel", [P, E * P], F16)
        b2bd = sb("b2bd", [P, J * D])
        gate_sb = sb("gate_sb", [E, D])
        gateT = sb("gateT", [P, E])
        wq_sb = sb("wq_sb", [P, 3, D])
        wqT = sb("wqT", [P, 3, D])
        wq2_sb = sb("wq2_sb", [P, 3, D])
        wf = sb("wf", [P, 3, D])
        wo_sb = sb("wo_sb", [P, D])
        bcol = sb("bcol", [P, 4])
        brow = sb("brow", [P, 5, D])
        bfold = sb("bfold", [P, 2, D])
        bvcol = sb("bvcol", [P, 1])
        amax = sb("amax", [P, 4])
        amax_all = sb("amax_all", [P, 4])
        scl = sb("scl", [P, 8])
        ident = sb("ident", [P, P])
        ident16 = sb("ident16", [P, P], F16)
        tri = sb("tri", [P, P])
        ones = sb("ones", [P, P])
        headmask = sb("headmask", [P, P])
        rev = sb("rev", [P, E])
        thr = sb("thr", [P, J])
        tnum = sb("tnum", [P, NTP])
        keep = sb("keep", [P, B * E * NC])
        z0 = sb("z0", [P, 64])

        st = sb("st", [P, B * J, 6])
        lnw = sb("lnw", [P, 8, B * J])
        lni = sb("lni", [P, B * J], I32)
        xn = sb("xn", [P, 2, J, D])
        xnT = sb("xnT", [P, L])
        xs = sb("xs", [P, B * J, 2 * D], F16)
        zl = sb("zl", [P, 4, B * J, E])
        small = sb("small", [P, 8, B * J])
        masks = sb("masks", [P, B, E, NC])
        incl = sb("incl", [P, B, E, NC])
        mpos = sb("mpos", [P, B, E, NC])
        cnt = sb("cnt", [P, 6, B, E])
        cmp = sb("cmp", [P, B, E, J])
        cmpt = sb("cmpt", [1, B, NTP, E])
        eidf = sb("eidf", [1, B, NTP])
        eids = sb("eids", [1, 2 * B * NTP], I32)
        posf = sb("posf", [P, 3, B, NC], I32)
        posr = sb("posr", [P, B, NC])
        rows = sb("rows", [P, 2 * B, NC], I32)
        g12 = sb("g12", [P, 2 * B, NC])
        gT = sb("gT", [P, 2, P])

        xsort = [sb(f"xsort{i}", [P, NT, 2 * D], F16) for i in range(2)]
        xT = sb("xT", [P, 2, 2 * P], F16)
        hh = sb("hh", [P, 2, F], F16)
        hl = sb("hl", [P, 2, F], F16)
        yall = sb("yall", [P, NT, D])
        yg = wraw2[:, 0:NC * D].rearrange("p (c d) -> p c d", c=NC)
        qk = wraw2[:, NC * D:].rearrange("p (i j d) -> p i j d", i=2, j=J)
        xaT, vT = wraw[:, 0:L], wraw[:, L:2 * L]
        tmp = wraw[:, 2 * L:].rearrange("p (i j d) -> p i j d", i=2, j=J)
        sbd = sb("sbd", [P, P])
        qks = sb("qks", [P, J, H])
        rq = sb("rq", [P, J, H])

        LB = [ps(f"LB{i}", [P, 512]) for i in range(4)]
        xTp = ps("xTp", [P, 1024], F16)
        hp = [ps(f"hp{i}", [P, 512]) for i in range(2)]
        yp = ps("yp", [P, 512])

        def xb(b):
            return x[:, b * J:(b + 1) * J, :]

        def lb3(i):
            return LB[i][:, :].rearrange("p (j d) -> p j d", j=4)

        PLAN = [("R", 0, [0, 1, 2, 3]), ("C", 0), ("C", 1), ("C", 2), ("M", 0), ("M", 1), ("R", 1, [0, 1]),
                ("C", 3), ("C", 4), ("M", 2), ("M", 3), ("R", 1, [2, 3]), ("C", 5), ("F", 0), ("C", 6),
                ("F", 1), ("C", 7), ("F", 2), ("F", 3)]
        SPLIT = [(0, 5), (5, 13), (13, NT)]

        def r_index(f, bs):
            return 0 if f == 0 else 1 + bs[0] // 2

        def stats_count(kind, f, bs):
            n = 0
            for job in PLAN:
                if job[0] == "R":
                    n += 1
                    if kind == "R" and (f, bs) == job[1:]:
                        return n
                if job[0] == "M":
                    if kind == "M" and f == job[1]:
                        return n + 1 + bs
                    n += 2

        def steps(engine, first, step):
            first()
            step(0)
            with engine.Fori(1, NT - 3, 2) as t:
                step(t)
                step(t + 1, odd=0)
            step(NT - 2)
            step(NT - 1)

        block = ctx.enter_context(nc.Block())

        @block.sync
        def _(sp):
            for b in range(B):
                sp.dma_start(xb(b), A_x[b].rearrange("(p j) h -> p j h", j=J)).then_inc(s_x_in, 16)
            sp.dma_start(gate_sb[:], gate_w).then_inc(s_gate_in, 16)
            sp.dma_start(wraw[:].rearrange("p (e f) -> p e f", e=E), w1.rearrange("e p f -> p e f")).then_inc(s_w1_in, 16)
            for r in (0, 32):
                sp.dma_start(b1raw[r:r + E, :], b1).then_inc(s_b1_in, 16)
            sp.dma_start(wraw2[:].rearrange("p (e c d) -> p e c d", e=E, c=FC),
                         w2.rearrange("e (c p) d -> p e c d", p=P)).then_inc(s_w2_in, 16)

            def load_slots(i):
                sp.wait_ge(scattered[i % B], 16 * NC * (i // B + 1))
                if i >= 2:
                    sp.wait_ge(s_xT_ps, NT * (i - 1))
                else:
                    sp.wait_ge(s_xs_zeroed, 16 * B)
                src = xs_dram[i % B].rearrange("(p t) c -> p t c", t=NT)
                for (lo, hi), landed in zip(SPLIT, slots_in[i % 2]):
                    sp.dma_start(xsort[i % 2][:, lo:hi, :], src[:, lo:hi, :]).then_inc(landed, 16)

            def store_slots(i):
                dst = y_dram[i % B].rearrange("(p t) c -> p t c", t=NT)
                for lo, hi in SPLIT:
                    sp.wait_ge(s_y_sb, NT * i + hi)
                    sp.dma_start(dst[:, lo:hi, :], yall[:, lo:hi, :]).then_inc(s_y_stored, 16)

            load_slots(0)
            load_slots(1)
            for i in range(2 * B):
                store_slots(i)
                if i + 2 < 2 * B:
                    load_slots(i + 2)
            for b in range(B):
                sp.wait_ge(s_comb, B + b + 1)
                sp.dma_start(out[b].rearrange("(p j) h -> p j h", j=J), xb(b)).then_inc(s_out_stored, 16)
            sp.wait_ge(s_out_stored, 16 * B)

        @block.gpsimd
        def _(pool):
            g = nc.gpsimd
            n = 0

            def order(ins):
                nonlocal n
                n += 1
                ins.then_inc(s_consts, 1)
                pool.wait_ge(s_consts, n)

            order(g.memset(ones[:], 1.0))
            order(g.affine_select(ident[:], ones[:], [[-1, P]], ALU.is_equal, 0.0, base=0, channel_multiplier=1))
            order(g.affine_select(tri[:], ones[:], [[1, P]], ALU.is_gt, 0.0, base=0, channel_multiplier=-1))
            hm = headmask[:].rearrange("p (h e) -> p h e", e=DH)
            order(g.affine_select(hm, ones[:].rearrange("p (h e) -> p h e", e=DH), [[-DH, H], [0, DH]], ALU.is_ge, 0.0,
                                  base=0, channel_multiplier=1))
            order(g.affine_select(hm, hm, [[DH, H], [0, DH]], ALU.is_ge, 0.0, base=DH - 1, channel_multiplier=-1))
            order(g.iota(rev[:], [[-1, E]], base=E, channel_multiplier=0, allow_small_or_imprecise_dtypes=True))
            order(g.iota(thr[:], [[P, J]], base=0, channel_multiplier=0, allow_small_or_imprecise_dtypes=True))
            order(g.iota(tnum[:], [[1, NTP]], base=0, channel_multiplier=0, allow_small_or_imprecise_dtypes=True))
            order(g.memset(keep[:], 1.0))
            order(g.memset(keep[:].rearrange("p (g c) -> p g c", c=NC)[:, :, 0:1], 0.0))
            pool.wait_ge(s_zero_set, 1)
            for b in range(B):
                pool.dma_start(xs_dram[b].rearrange("(p t) c -> p t c", t=NT), xsort[0][:]).then_inc(s_xs_zeroed, 16)

            pool.wait_ge(s_b2_zero, 1)
            for r in range(2):
                for j in range(J):
                    k = r * 64 + j * E
                    pool.dma_start(b2bd[k:k + E, j * D:(j + 1) * D], b2).then_inc(s_b2_in, 16)

            pool.wait_ge(s_absmax, 1)
            g.partition_all_reduce(amax_all[:, 0:2], amax[:, 0:2], P, RMAX).then_inc(s_absmax_all, 1)
            pool.wait_ge(s_absmax, 2)
            g.partition_all_reduce(amax_all[:, 2:3], amax[:, 2:3], P, RMAX).then_inc(s_absmax_all, 1)

            def scatter(i):
                b = i % B
                pool.wait_ge(s_pos, i + 1)
                pool.wait_ge(s_xs_rows, i + 1)
                if i == 0:
                    pool.wait_ge(s_xs_zeroed, 16 * B)
                for c in range(NC):
                    g.indirect_dma_start(
                        out=xs_dram[b], out_offset=bass.IndirectOffsetOnAxis(ap=rows[:, i, c:c + 1], axis=0),
                        in_=xs[:, b * J + c % J, :], in_offset=None).then_inc(scattered[b], 16)

            def gather(i):
                b = i % B
                pool.wait_ge(s_y_stored, 16 * len(SPLIT) * (i + 1))
                if i:
                    pool.wait_ge(s_comb, i)
                for c in range(NC):
                    g.indirect_dma_start(
                        out=yg[:, c, :], out_offset=None, in_=y_dram[b],
                        in_offset=bass.IndirectOffsetOnAxis(ap=rows[:, i, c:c + 1], axis=0)).then_inc(s_gathered, 16)

            for i in range(B):
                scatter(i)
            gather(0)
            gather(1)
            scatter(4)
            scatter(5)
            gather(2)
            gather(3)
            scatter(6)
            scatter(7)
            for i in range(B, 2 * B):
                gather(i)

        @block.tensor
        def _(pe):
            mm, tr = nc.tensor.matmul, nc.tensor.transpose

            def setup():
                pe.wait_ge(s_consts, 10)
                pe.wait_ge(s_gate_in, 16)
                tr(LB[0][:, 0:E], gate_sb[:], ident[0:E, 0:E]).then_inc(s_gate_ps, 1)

            def fold():
                pe.wait_ge(s_wqkv_in, 16 * 3)
                for i in range(3):
                    last = tr(LB[1][:, i * D:(i + 1) * D], wq_sb[:, i, :], ident[:])
                last.then_inc(s_wT_ps, 1)
                pe.wait_ge(s_wT_sb, 1)
                pe.wait_ge(s_wqkv2_in, 16 * 3)
                for i in range(3):
                    last = mm(LB[1][:, i * D:(i + 1) * D], wqT[:, i, :], wq2_sb[:, i, :], start=True, stop=True)
                last.then_inc(s_wf_ps, 1)

            def fold_biases():
                pe.wait_ge(s_bcol_in, 16 * 4)
                for i in range(2):
                    mm(LB[3][:, i * D:(i + 1) * D], bcol[:, i:i + 1].broadcast_to([P, P]), wq2_sb[:, i, :], start=True, stop=True)
                mm(LB[3][:, 2 * D:2 * D + 1], wq2_sb[:, 2, :], bcol[:, 2:3], start=True, stop=True).then_inc(s_bf_ps, 1)

            def route(f, bs):
                for b in bs:
                    i = f * B + b
                    pe.wait_ge(s_xn, i + 1)
                    if i:
                        pe.wait_ge(s_xnT_sb, i)
                    if i == 0:
                        pe.wait_ge(s_gate_sb, 1)
                    if i == 1:
                        pe.wait_ge(s_wf_sb, 1)
                    if b == bs[0] and f:
                        pe.wait_ge(s_x2, bs[-1] + 1)
                    for j in range(J):
                        last = tr(LB[j // 4][:, (j % 4) * P:(j % 4 + 1) * P], xn[:, b % 2, j, :], ident[:])
                    last.then_inc(s_xnT_ps, 1)
                    pe.wait_ge(s_xnT_sb, i + 1)
                    for j in range(J):
                        last = mm(LB[2][:, (b * J + j) * E:(b * J + j + 1) * E], xnT[:, j * P:(j + 1) * P], gateT[:],
                                  start=True, stop=True)
                    last.then_inc(s_logits, 1)
                    if i == 0:
                        fold()
                q = r_index(f, bs)
                pe.wait_ge(s_tile_counts, q + 1)
                for k, lhs in enumerate((tri, ones)):
                    for b in bs:
                        last = mm(LB[3][:, (k * B + b) * E:(k * B + b + 1) * E], lhs[:], incl[:, b, :, NC - 1],
                                  start=True, stop=True)
                last.then_inc(s_prefix, 1)
                pe.wait_ge(s_gates, q + 1)
                pe.wait_ge(s_eids, q + 1)
                for h in range(len(bs) // 2):
                    b = bs[2 * h]
                    last = tr(LB[3][:, h * P:(h + 1) * P], zl[:, 3, b * J:(b + 2) * J, :].rearrange("p j e -> p (j e)"), ident[:])
                last.then_inc(s_gT_ps, 1)
                pe.wait_ge(s_gT_sb, q + 1)
                if f == 0:
                    pe.wait_ge(s_b2_in, 16 * 2 * J)
                for b in bs:
                    h, r = (b - bs[0]) // 2, 64 * (b % 2)
                    if b != bs[0]:
                        pe.wait_ge(s_b2_added, f * B + b)
                    for k in range(2):
                        last = mm(LB[k][:], gT[r:r + 64, h, :], b2bd[r:r + 64, k * 512:(k + 1) * 512], start=True, stop=True)
                    last.then_inc(s_b2_ps, 1)
                if f == 0:
                    fold_biases()

            def ffn(i):
                g0 = i * NT
                buf = xsort[i % 2]

                def turn(t, p):
                    if not (isinstance(t, int) and g0 + t == 0):
                        pe.wait_ge(s_xT_sb, g0 + t)
                    for k in range(2):
                        if isinstance(t, int):
                            src = buf[:, t, k * D:(k + 1) * D]
                        else:
                            src = buf[:].rearrange("p t c -> p (t c)")[:, bass.ds(t * (2 * D) + k * D, D)]
                        last = tr(xTp[:, k * P:(k + 1) * P], src, ident16[:])
                    last.then_inc(s_xT_ps, 1)

                def expert(t):
                    return pe.value_load(eids[0:1, bass.ds(t + i * NTP, 1)], min_val=0, max_val=E - 1)

                def up(t, p):
                    e = expert(t)
                    pe.wait_ge(s_xT_sb, g0 + t + 1)
                    if not (isinstance(t, int) and g0 + t < 2):
                        pe.wait_ge(s_h_lo, g0 + t - 1)
                    hi, lo = xT[:, p, 0:P], xT[:, p, P:2 * P]
                    for c in range(FC):
                        o = hp[p][:, c * P:(c + 1) * P]
                        wh = w1s[:, bass.ds(e * (2 * F) + c * P, P)]
                        wl = w1s[:, bass.ds(e * (2 * F) + F + c * P, P)]
                        mm(o, b1s[:, c * P:(c + 1) * P], sel[:, bass.ds(e * P, P)], start=True, stop=False)
                        mm(o, wh, hi, start=False, stop=False)
                        mm(o, wh, lo, start=False, stop=False)
                        last = mm(o, wl, hi, start=False, stop=True)
                    last.then_inc(s_h_ps, 1)

                def down(t, p):
                    e = expert(t)
                    pe.wait_ge(s_h_lo, g0 + t + 1)
                    if not (isinstance(t, int) and g0 + t == 0):
                        pe.wait_ge(s_y_sb, g0 + t)
                    for c in range(FC):
                        wh = w2s[:, bass.ds(e * (2 * F) + c * P, P)]
                        wl = w2s[:, bass.ds(e * (2 * F) + F + c * P, P)]
                        h1, h2 = hh[:, p, c * P:(c + 1) * P], hl[:, p, c * P:(c + 1) * P]
                        mm(yp[:, 0:D], h1, wh, start=(c == 0), stop=False)
                        mm(yp[:, 0:D], h1, wl, start=False, stop=False)
                        last = mm(yp[:, 0:D], h2, wh, start=False, stop=(c == FC - 1))
                    last.then_inc(s_y_ps, 1)

                def first():
                    pe.wait_ge(s_eids, 1 if i < B else (2 if i < 6 else 3))
                    if i == 0:
                        pe.wait_ge(s_w1_hi, 1)
                        pe.wait_ge(s_w1_lo, 1)
                        pe.wait_ge(s_b1_lo, 1)
                        pe.wait_ge(s_sel16, 1)
                    for landed in slots_in[i % 2]:
                        pe.wait_ge(landed, 16 * (i // 2 + 1))
                    turn(0, 0)
                    turn(1, 1)
                    if i:
                        pe.wait_ge(s_h_lo, g0)
                    up(0, 0)
                    if i == 0:
                        pe.wait_ge(s_w2_hi, 1)
                        pe.wait_ge(s_w2_lo, 1)

                def step(t, odd=None):
                    p = t % 2 if isinstance(t, int) else (1 if odd is None else odd)
                    if not isinstance(t, int) or t + 2 < NT:
                        turn(t + 2, p)
                    if not isinstance(t, int) or t + 1 < NT:
                        up(t + 1, 1 - p)
                    down(t, p)

                steps(pe, first, step)

            def attend(b):
                pe.wait_ge(s_xa, b + 1)
                for j in range(J):
                    last = tr(LB[j // 4][:, (j % 4) * P:(j % 4 + 1) * P], tmp[:, 0, j, :], ident[:])
                last.then_inc(s_xaT_ps, 1)
                pe.wait_ge(s_xaT_sb, b + 1)
                for k in range(2):
                    last = mm(LB[k][:], wf[:, 2, :], xaT[:, k * 512:(k + 1) * 512], start=True, stop=True)
                last.then_inc(s_v_ps, 1)
                for j in range(J):
                    last = mm(LB[2 + j // 4][:, (j % 4) * D:(j % 4 + 1) * D], xaT[:, j * P:(j + 1) * P], wf[:, 1, :],
                              start=True, stop=True)
                last.then_inc(s_k_ps, 1)
                pe.wait_ge(s_v_sb, b + 1)
                for j in range(J):
                    last = mm(LB[j // 4][:, (j % 4) * D:(j % 4 + 1) * D], xaT[:, j * P:(j + 1) * P], wf[:, 0, :],
                              start=True, stop=True)
                last.then_inc(s_q_ps, 1)
                pe.wait_ge(s_zk, b + 1)
                pe.wait_ge(s_fq, b + 1)
                pe.wait_ge(s_fk, b + 1)
                for j in range(J):
                    last = mm(LB[2][:, 0:P], qk[:, 1, j, :], qk[:, 0, j, :], start=(j == 0), stop=(j == J - 1))
                last.then_inc(s_s_ps, 1)
                pe.wait_ge(s_s_sb, b + 1)
                for j in range(J):
                    last = mm(LB[j // 4][:, (j % 4) * D:(j % 4 + 1) * D], vT[:, j * P:(j + 1) * P], sbd[:], start=True, stop=True)
                last.then_inc(s_o_ps, 1)
                pe.wait_ge(s_o_sb, b + 1)
                for j in range(J):
                    last = tr(LB[j // 4][:, (j % 4) * P:(j % 4 + 1) * P], tmp[:, 1, j, :], ident[:])
                last.then_inc(s_oT_ps, 1)
                pe.wait_ge(s_oT_sb, b + 1)
                for j in range(J):
                    last = mm(LB[2 + j // 4][:, (j % 4) * D:(j % 4 + 1) * D], xaT[:, j * P:(j + 1) * P], wo_sb[:], start=True, stop=True)
                last.then_inc(s_wo_ps, 1)

            setup()
            for job in PLAN:
                if job[0] == "R":
                    route(job[1], job[2])
                elif job[0] == "C":
                    ffn(job[1])
                elif job[0] == "M":
                    if job[1] == 0:
                        pe.wait_ge(s_wf_sb, 1)
                        pe.wait_ge(s_bf_sb, 1)
                        pe.wait_ge(s_wo_in, 16)
                        pe.wait_ge(s_b2_added, B)
                    attend(job[1])

        @block.scalar
        def _(act):
            a = nc.scalar.activation

            def setup():
                for i, w in enumerate((Wq, Wk, Wv)):
                    act.dma_start(wq_sb[:, i, :], w).then_inc(s_wqkv_in, 16)
                for i, w in enumerate((Wq2, Wk2, Wv2)):
                    act.dma_start(wq2_sb[:, i, :], w).then_inc(s_wqkv2_in, 16)
                act.dma_start(wo_sb[:], Wo).then_inc(s_wo_in, 16)
                for i, v in enumerate((bq, bk, bv, bv2)):
                    act.dma_start(bcol[:, i:i + 1], v.rearrange("(p a) -> p a", a=1)).then_inc(s_bcol_in, 16)
                for i, v in enumerate((bq2, bk2, bo, gamma, beta)):
                    act.dma_start(brow[:, i, :], v.rearrange("(a d) -> a d", a=1).broadcast_to([P, D])).then_inc(s_brow_in, 16)
                act.wait_ge(s_gate_ps, 1)
                a(gateT[:], LB[0][:, 0:E], ACT.Copy).then_inc(s_gate_sb, 1)

            def fold():
                act.wait_ge(s_wT_ps, 1)
                a(wqT[:].rearrange("p i d -> p (i d)"), LB[1][:, 0:3 * D], ACT.Copy).then_inc(s_wT_sb, 1)
                act.wait_ge(s_wf_ps, 1)
                a(wf[:].rearrange("p i d -> p (i d)"), LB[1][:, 0:3 * D], ACT.Copy).then_inc(s_wf_sb, 1)

            def split_weights():
                act.wait_ge(s_scales, 1)
                act.wait_ge(s_w1_in, 16)
                a(w1s[:].rearrange("p (e k f) -> p e k f", e=E, k=2)[:, :, 0, :], wraw[:].rearrange("p (e f) -> p e f", e=E),
                  ACT.Copy, scale=scl[:, 0:1]).then_inc(s_w1_hi, 1)
                act.wait_ge(s_b1_in, 32)
                a(b1s[0:E, :], b1raw[0:E, :], ACT.Copy, scale=scl[0:E, 2:3])
                a(b1h[32:40, :], b1raw[32:40, :], ACT.Copy, scale=scl[32:40, 2:3]).then_inc(s_b1_hi, 1)
                act.wait_ge(s_scales, 2)
                act.wait_ge(s_w2_in, 16)
                a(w2s[:].rearrange("p (e k f) -> p e k f", e=E, k=2)[:, :, 0, :], wraw2[:].rearrange("p (e f) -> p e f", e=E),
                  ACT.Copy, scale=scl[:, 1:2]).then_inc(s_w2_hi, 1)

            def normalise(dst, src, lo, last_sem):
                for j in range(J):
                    last = a(dst[:, j, :], src[:, j, :], ACT.Identity, scale=lnw[:, 5, lo + j:lo + j + 1],
                             bias=lnw[:, 6, lo + j:lo + j + 1])
                last.then_inc(last_sem, 1)

            def evacuate(dst, banks, sem):
                for k in range(2):
                    last = a(dst[:, k * 512:(k + 1) * 512], LB[banks + k][:], ACT.Copy)
                last.then_inc(sem, 1)

            def route(f, bs):
                q = r_index(f, bs)
                act.wait_ge(s_ln_stats, stats_count("R", f, bs))
                for b in bs:
                    i = f * B + b
                    if i >= 2:
                        act.wait_ge(s_xnT_ps, i - 1)
                        act.wait_ge(s_xs_rows, i - 1)
                    normalise(xn[:, b % 2], xb(b), b * J, s_xn)
                    act.wait_ge(s_xn, i + 1)
                    if f:
                        act.wait_ge(scattered[b], 16 * NC)
                    a(xs[:, b * J:(b + 1) * J, 0:D], xn[:, b % 2], ACT.Copy, scale=XS).then_inc(s_xhi, 1)
                    act.wait_ge(s_xnT_ps, i + 1)
                    if i:
                        act.wait_ge(s_logits, i)
                    evacuate(xnT, 0, s_xnT_sb)
                    if i == 0:
                        fold()
                if f == 0:
                    split_weights()
                act.wait_ge(s_zs, q + 1)
                lo, hi = bs[0] * J, (bs[-1] + 1) * J
                a(zl[:, 1, lo:hi, :], zl[:, 0, lo:hi, :], ACT.Exp).then_inc(s_ez, 1)
                act.wait_ge(s_z2, q + 1)
                a(small[:, 3, lo:hi], small[:, 2, lo:hi], ACT.Exp).then_inc(s_e2, 1)
                act.wait_ge(s_gT_ps, q + 1)
                n = len(bs) // 2 * P
                a(gT[:].rearrange("p h t -> p (h t)")[:, 0:n], LB[3][:, 0:n], ACT.Copy).then_inc(s_gT_sb, 1)

            def ffn(i):
                g0 = i * NT

                def high(t, p):
                    act.wait_ge(s_h_ps, g0 + t + 1)
                    if not (isinstance(t, int) and g0 + t < 2):
                        act.wait_ge(s_y_ps, g0 + t - 1)
                    if isinstance(t, int) and t == 0 and i:
                        act.wait_ge(s_y_ps, g0)
                    a(hh[:, p, :], hp[p][:], ACT.Relu).then_inc(s_h_hi, 1)

                def result(t, p):
                    act.wait_ge(s_y_ps, g0 + t + 1)
                    if isinstance(t, int) and t == 0 and i:
                        act.wait_ge(s_y_stored, 16 * len(SPLIT) * i)
                    if isinstance(t, int):
                        dst = yall[:, t, :]
                    else:
                        dst = yall[:].rearrange("p t c -> p (t c)")[:, bass.ds(t * D, D)]
                    a(dst, yp[:, 0:D], ACT.Copy).then_inc(s_y_sb, 1)

                def first():
                    high(0, 0)

                def step(t, odd=None):
                    p = t % 2 if isinstance(t, int) else (1 if odd is None else odd)
                    if not isinstance(t, int) or t + 1 < NT:
                        high(t + 1, 1 - p)
                    result(t, p)

                steps(act, first, step)

            def attend(b):
                act.wait_ge(s_ln_stats, stats_count("M", b, 0))
                normalise(tmp[:, 0], xb(b), b * J, s_xa)
                act.wait_ge(s_xaT_ps, b + 1)
                evacuate(xaT, 0, s_xaT_sb)
                act.wait_ge(s_v_ps, b + 1)
                if b == 0:
                    act.wait_ge(s_bf_sb, 1)
                for k in range(2):
                    last = a(vT[:, k * 512:(k + 1) * 512], LB[k][:], ACT.Identity, bias=bvcol[:])
                last.then_inc(s_v_sb, 1)
                act.wait_ge(s_zk, b + 1)
                a(xn[:, 1], xn[:, 1], ACT.Exp).then_inc(s_ek, 1)
                act.wait_ge(s_zq, b + 1)
                a(xn[:, 0], xn[:, 0], ACT.Exp).then_inc(s_eq, 1)
                act.wait_ge(s_oT_ps, b + 1)
                evacuate(xaT, 0, s_oT_sb)
                act.wait_ge(s_ln_stats, stats_count("M", b, 1))
                normalise(tmp[:, 1], qk[:, 0], b * J, s_yn)

            setup()
            for job in PLAN:
                if job[0] == "R":
                    route(job[1], job[2])
                elif job[0] == "C":
                    ffn(job[1])
                elif job[0] == "M":
                    attend(job[1])

        @block.vector
        def _(dve):
            v = nc.vector
            n = 0

            def link(ins):
                nonlocal n
                n += 1
                ins.then_inc(s_dve_order, 1)
                dve.wait_ge(s_dve_order, n)

            def setup():
                v.memset(xsort[0][:].rearrange("p t c -> p (t c)").bitcast(U32), 0).then_inc(s_zero_set, 1)
                v.memset(b2bd[:], 0.0).then_inc(s_b2_zero, 1)
                link(v.memset(b1s[:].bitcast(U32), 0))
                v.memset(amax[:], 0.0)
                dve.wait_ge(s_consts, 10)
                link(v.tensor_copy(ident16[:], ident[:]))
                v.tensor_tensor(sel[:].rearrange("p (e t) -> p e t", e=E), ident16[:, 0:E].unsqueeze(2).broadcast_to([P, E, P]),
                                ident16[:, 32:32 + E].unsqueeze(2).broadcast_to([P, E, P]), ALU.add).then_inc(s_sel16, 1)

            def weight_scales():
                dve.wait_ge(s_w1_in, 16)
                v.tensor_reduce(amax[:, 0:1], wraw[:], AX, ALU.max, apply_absolute_value=True)
                dve.wait_ge(s_b1_in, 32)
                v.tensor_reduce(amax[0:E, 1:2], b1raw[0:E, :], AX, ALU.max, apply_absolute_value=True).then_inc(s_absmax, 1)
                dve.wait_ge(s_absmax_all, 1)
                link(v.scalar_tensor_tensor(scl[:, 4:5], amax_all[:, 0:1], float(D), amax_all[:, 1:2], ALU.mult, ALU.max))
                power(4, 0, 2.0 ** 8)
                v.tensor_scalar(scl[:, 2:3], scl[:, 0:1], XS, None, ALU.mult).then_inc(s_scales, 1)

            def power(src, dst, by):
                link(v.tensor_scalar(scl[:, src:src + 1], scl[:, src:src + 1], 1e-30, 1e30, ALU.max, ALU.min))
                bits = scl[:].bitcast(U32)
                link(v.tensor_scalar(bits[:, src:src + 1], bits[:, src:src + 1], 0x7F800000, 0x7F800000,
                                     ALU.bitwise_and, ALU.bitwise_xor))
                link(v.tensor_scalar(scl[:, dst:dst + 1], scl[:, src:src + 1], by, None, ALU.mult))

            def weight_lows():
                dve.wait_ge(s_w1_hi, 1)
                w = w1s[:].rearrange("p (e k f) -> p e k f", e=E, k=2)
                raw = wraw[:].rearrange("p (e f) -> p e f", e=E)
                v.scalar_tensor_tensor(w[:, :, 1, :], raw, scl[:, 0:1], w[:, :, 0, :], ALU.mult, ALU.subtract).then_inc(s_w1_lo, 1)
                dve.wait_ge(s_b1_hi, 1)
                v.scalar_tensor_tensor(b1s[32:40, :], b1raw[32:40, :], scl[32:40, 2:3], b1h[32:40, :], ALU.mult,
                                       ALU.subtract).then_inc(s_b1_lo, 1)
                dve.wait_ge(s_w2_in, 16)
                v.tensor_reduce(amax[:, 2:3], wraw2[:], AX, ALU.max, apply_absolute_value=True).then_inc(s_absmax, 1)
                dve.wait_ge(s_absmax_all, 2)
                link(v.tensor_copy(scl[:, 5:6], amax_all[:, 2:3]))
                power(5, 1, 2.0 ** 12)
                link(v.tensor_tensor(scl[:, 6:7], scl[:, 1:2], scl[:, 2:3], ALU.mult))
                link(v.reciprocal(scl[:, 3:4], scl[:, 6:7]))
                v.tensor_scalar(scl[:, 3:4], scl[:, 3:4], 0.5, None, ALU.mult).then_inc(s_scales, 1)
                dve.wait_ge(s_w2_hi, 1)
                w = w2s[:].rearrange("p (e k f) -> p e k f", e=E, k=2)
                raw = wraw2[:].rearrange("p (e f) -> p e f", e=E)
                v.scalar_tensor_tensor(w[:, :, 1, :], raw, scl[:, 1:2], w[:, :, 0, :], ALU.mult, ALU.subtract).then_inc(s_w2_lo, 1)

            def statistics(src, lo, m, eps):
                for j in range(m):
                    last = v.bn_stats(st[:, lo + j, :], src[:, j, :])
                link(last)
                W = [lnw[:, k, lo:lo + m] for k in range(8)]
                me, qe, mo, qo = (st[:, lo:lo + m, k] for k in (1, 2, 4, 5))
                v.tensor_tensor(W[1], qe, qo, ALU.add)
                v.tensor_tensor(W[2], me, mo, ALU.add)
                link(v.tensor_tensor(W[0], me, mo, ALU.subtract))
                link(v.scalar_tensor_tensor(W[0], W[0], float(D // 4), W[0], ALU.mult, ALU.mult))
                link(v.tensor_tensor(W[0], W[0], W[1], ALU.add))
                link(v.tensor_scalar(W[0], W[0], 1.0 / D, eps, ALU.mult, ALU.add))
                ib = lni[:, lo:lo + m]
                link(v.tensor_scalar(ib, W[0].bitcast(I32), 1, None, ALU.logical_shift_right))
                link(v.tensor_scalar(W[5].bitcast(I32), ib, -1.0, float(0x5F3759DF), ALU.mult, ALU.add))
                for _ in range(3):
                    link(v.scalar_tensor_tensor(W[3], W[5], -0.5, W[5], ALU.mult, ALU.mult))
                    link(v.tensor_tensor(W[3], W[3], W[0], ALU.mult))
                    link(v.scalar_tensor_tensor(W[5], W[3], 1.5, W[5], ALU.add, ALU.mult))
                v.scalar_tensor_tensor(W[6], W[2], -0.5, W[5], ALU.mult, ALU.mult).then_inc(s_ln_stats, 1)

            def rowsplit(f, b):
                i = f * B + b
                dve.wait_ge(s_xhi, i + 1)
                dst = xs[:, b * J:(b + 1) * J, :]
                v.scalar_tensor_tensor(dst[:, :, D:2 * D], xn[:, b % 2], XS, dst[:, :, 0:D], ALU.mult,
                                       ALU.subtract).then_inc(s_xs_rows, 1)

            def route(f, bs):
                q, nb = r_index(f, bs), len(bs)
                lo, hi, m = bs[0] * J, (bs[-1] + 1) * J, nb * J
                b0, b1_ = bs[0], bs[-1] + 1
                if f == 0:
                    dve.wait_ge(s_x_in, 16 * B)
                statistics(x[:, lo:hi, :], lo, m, EPS_FFN)
                if f == 0:
                    weight_scales()
                for b in bs:
                    rowsplit(f, b)
                if f == 0:
                    weight_lows()
                Z, EZ, T, G = (zl[:, k, lo:hi, :] for k in range(4))
                m1, s1, m2, e2, c1, rs, g1, c2 = (small[:, k, lo:hi] for k in range(8))

                def each(a):
                    return a.unsqueeze(2).broadcast_to([P, m, E])
                revb = rev[:].unsqueeze(1).broadcast_to([P, m, E])
                dve.wait_ge(s_logits, f * B + bs[-1] + 1)
                lg = LB[2][:, lo * E:hi * E].rearrange("p (j e) -> p j e", e=E)
                link(v.tensor_reduce(m1, lg, AX, ALU.max))
                v.tensor_tensor(Z, lg, each(m1), ALU.subtract).then_inc(s_zs, 1)
                dve.wait_ge(s_zs, q + 1)

                def first_of(eqm, k):
                    link(v.tensor_tensor(eqm, eqm, revb, ALU.mult))
                    link(v.tensor_reduce(c1, eqm, AX, ALU.max))
                    for b in bs:
                        r = slice((b - b0) * J, (b - b0 + 1) * J)
                        mk = masks[:, b, :, k * J:(k + 1) * J].rearrange("p e j -> p j e")
                        last = v.tensor_tensor(mk, eqm[:, r, :], each(c1)[:, r, :], ALU.is_equal)
                    link(last)

                def mask(b, k):
                    return masks[:, b, :, k * J:(k + 1) * J].rearrange("p e j -> p j e")

                link(v.tensor_scalar(T, Z, 0.0, None, ALU.is_ge))
                first_of(T, 0)
                for b in bs:
                    r = slice((b - b0) * J, (b - b0 + 1) * J)
                    last = v.scalar_tensor_tensor(T[:, r, :], mask(b, 0), -3.0e38, Z[:, r, :], ALU.mult, ALU.add)
                link(last)
                v.tensor_reduce(m2, T, AX, ALU.max).then_inc(s_z2, 1)
                dve.wait_ge(s_z2, q + 1)
                link(v.tensor_tensor(T, T, each(m2), ALU.is_equal))
                first_of(T, 1)
                mf, inf, kf = (t[:].rearrange("p b e c -> p (b e c)") for t in (masks, incl, masks))
                w0, w1_ = b0 * E * NC, b1_ * E * NC
                v.tensor_tensor_scan(inf[:, w0:w1_], keep[:, 0:w1_ - w0], mf[:, w0:w1_], 0.0, ALU.mult, ALU.add)\
                    .then_inc(s_tile_counts, 1)
                dve.wait_ge(s_ez, q + 1)
                link(v.tensor_reduce(s1, EZ, AX, ALU.add))
                link(v.reciprocal(rs, s1))
                link(v.tensor_scalar(s1, rs, 0.5, None, ALU.mult))
                dve.wait_ge(s_e2, q + 1)
                link(v.tensor_tensor(e2, e2, s1, ALU.mult))
                for b in bs:
                    r = slice((b - b0) * J, (b - b0 + 1) * J)
                    i = f * B + b
                    v.tensor_tensor(G[:, r, :], mask(b, 0), each(s1)[:, r, :], ALU.mult)
                    v.tensor_tensor(T[:, r, :], mask(b, 1), each(e2)[:, r, :], ALU.mult)
                    v.tensor_scalar(g12[:, i, 0:J], s1[:, r], scl[:, 3:4], 2.0, ALU.mult, ALU.mult)
                    last = v.tensor_scalar(g12[:, i, J:NC], e2[:, r], scl[:, 3:4], 2.0, ALU.mult, ALU.mult)
                link(last)
                v.tensor_tensor(G, G, T, ALU.add).then_inc(s_gates, 1)
                dve.wait_ge(s_prefix, q + 1)
                C = [cnt[:, k, b0:b1_, :] for k in range(6)]
                base = LB[3][:, b0 * E:b1_ * E].rearrange("p (b e) -> p b e", e=E)
                total = LB[3][:, (B + b0) * E:(B + b1_) * E].rearrange("p (b e) -> p b e", e=E)
                v.tensor_copy(C[4], base)
                cm = cmp[:, b0:b1_, :, :]
                for b in bs:
                    last = v.tensor_tensor(cmp[:, b], total[:, b - b0, :].unsqueeze(2).broadcast_to([P, E, J]),
                                           thr[:].unsqueeze(1).broadcast_to([P, E, J]), ALU.is_gt)
                link(last)
                link(v.tensor_reduce(C[0].rearrange("p b e -> p (b e)"), cm.rearrange("p b e k -> p (b e) k"), AX, ALU.add))
                for b in bs:
                    last = v.tensor_tensor_scan(cnt[:, 1, b, :], ones[:, 0:E], cnt[:, 0, b, :], 0.0, ALU.mult, ALU.add)
                link(last)
                link(v.scalar_tensor_tensor(C[2], C[0], -float(P), C[4], ALU.mult, ALU.add))
                link(v.scalar_tensor_tensor(C[3], C[1], float(P), C[2], ALU.mult, ALU.add))
                for b in bs:
                    last = v.tensor_tensor(cmpt[:, b], cnt[0:1, 1, b, :].unsqueeze(1).broadcast_to([1, NTP, E]),
                                           tnum[0:1, :].unsqueeze(2).broadcast_to([1, NTP, E]), ALU.is_le)
                link(last)
                link(v.tensor_reduce(eidf[:, b0:b1_, :].rearrange("p b t -> p (b t)"),
                                     cmpt[:, b0:b1_].rearrange("p b t e -> p (b t) e"), AX, ALU.add))
                e0 = (f * B + b0) * NTP
                v.tensor_scalar(eids[:, e0:e0 + nb * NTP], eidf[:, b0:b1_, :].rearrange("p b t -> p (b t)"), float(E - 1), None,
                                ALU.min).then_inc(s_eids, 1)
                for b in bs:
                    i = f * B + b
                    link(v.tensor_tensor(mpos[:, b], incl[:, b], cnt[:, 3, b, :].unsqueeze(2).broadcast_to([P, E, NC]), ALU.add))
                    link(v.tensor_tensor(mpos[:, b], mpos[:, b], masks[:, b], ALU.mult))
                    link(v.tensor_reduce(posr[:, b, :], mpos[:, b].rearrange("p e c -> p c e"), AX, ALU.add))
                    link(v.tensor_scalar(posf[:, 0, b, :], posr[:, b, :], -1.0, float(SLOTS - 1), ALU.add, ALU.min))
                    v.tensor_scalar(posf[:, 1, b, :], posf[:, 0, b, :], 7, None, ALU.logical_shift_right)
                    link(v.tensor_scalar(posf[:, 2, b, :], posf[:, 0, b, :], P - 1, None, ALU.bitwise_and))
                    v.scalar_tensor_tensor(rows[:, i, :], posf[:, 2, b, :], float(NT), posf[:, 1, b, :], ALU.mult,
                                           ALU.add).then_inc(s_pos, 1)
                for b in bs:
                    i = f * B + b
                    dve.wait_ge(s_b2_ps, i + 1)
                    for k in range(2):
                        last = v.tensor_tensor(xb(b)[:, 4 * k:4 * k + 4, :], xb(b)[:, 4 * k:4 * k + 4, :], lb3(k), ALU.add)
                    last.then_inc(s_b2_added, 1)

            def ffn(i):
                g0 = i * NT

                def columns(t, p):
                    dve.wait_ge(s_xT_ps, g0 + t + 1)
                    if not (isinstance(t, int) and g0 + t < 2):
                        dve.wait_ge(s_h_ps, g0 + t - 1)
                    if isinstance(t, int) and t == 0 and i:
                        dve.wait_ge(s_h_ps, g0)
                    v.tensor_copy(xT[:, p, :], xTp[:, 0:2 * P]).then_inc(s_xT_sb, 1)

                def low(t, p):
                    dve.wait_ge(s_h_hi, g0 + t + 1)
                    v.scalar_tensor_tensor(hl[:, p, :], hp[p][:], 0.0, hh[:, p, :], ALU.max, ALU.subtract).then_inc(s_h_lo, 1)

                def first():
                    columns(0, 0)
                    columns(1, 1)
                    low(0, 0)

                def step(t, odd=None):
                    p = t % 2 if isinstance(t, int) else (1 if odd is None else odd)
                    if not isinstance(t, int) or t + 2 < NT:
                        columns(t + 2, p)
                    if not isinstance(t, int) or t + 1 < NT:
                        low(t + 1, 1 - p)

                steps(dve, first, step)

            def combine(i, done=None):
                b = i % B
                dve.wait_ge(s_gathered, 16 * NC * (i + 1))
                for k in range(TOPK):
                    for j in range(J):
                        c = k * J + j
                        last = v.scalar_tensor_tensor(xb(b)[:, j, :], yg[:, c, :], g12[:, i, c:c + 1], xb(b)[:, j, :],
                                                      ALU.mult, ALU.add)
                    if k == 0:
                        link(last)
                last.then_inc(s_comb, 1)
                dve.wait_ge(s_comb, i + 1)

            def attend(b):
                combine(b)
                statistics(xb(b), b * J, J, EPS_FFN)
                for i, ready, bank, zsem in ((1, s_k_ps, 2, s_zk), (0, s_q_ps, 0, s_zq)):
                    dve.wait_ge(ready, b + 1)
                    for k in range(2):
                        last = v.tensor_tensor(qk[:, i, 4 * k:4 * k + 4, :], lb3(bank + k),
                                               bfold[:, i, :].unsqueeze(1).broadcast_to([P, 4, D]), ALU.add)
                    link(last)
                    v.tensor_scalar(xn[:, i], qk[:, i], 0.0, None, ALU.min).then_inc(zsem, 1)
                for i, ready, fsem in ((1, s_ek, s_fk), (0, s_eq, s_fq)):
                    dve.wait_ge(ready, b + 1)
                    v.scalar_tensor_tensor(qk[:, i], qk[:, i], 0.0, xn[:, i], ALU.max, ALU.add).then_inc(fsem, 1)
                dve.wait_ge(s_fq, b + 1)
                dve.wait_ge(s_fk, b + 1)
                link(v.tensor_tensor(tmp[:, 1], qk[:, 0], qk[:, 1], ALU.mult))
                link(v.tensor_reduce(qks[:], tmp[:, 1].rearrange("p j (h e) -> p j h e", e=DH), AX, ALU.add))
                link(v.tensor_scalar(qks[:], qks[:], EPS_QK, None, ALU.add))
                link(v.reciprocal(rq[:], qks[:]))
                dve.wait_ge(s_s_ps, b + 1)
                v.tensor_tensor(sbd[:], LB[2][:, 0:P], headmask[:], ALU.mult).then_inc(s_s_sb, 1)
                bob, betab, gammab = (brow[:, k, :].unsqueeze(1).broadcast_to([P, J, D]) for k in (2, 4, 3))
                v.tensor_tensor(tmp[:, 0], tmp[:, 0], bob, ALU.add)
                link(v.tensor_tensor(xb(b), xb(b), betab, ALU.add))
                dve.wait_ge(s_o_ps, b + 1)
                for k in range(2):
                    last = v.tensor_tensor(tmp[:, 1, 4 * k:4 * k + 4, :].rearrange("p j (h e) -> p (j h) e", e=DH),
                                           LB[k][:].rearrange("p (g e) -> p g e", e=DH),
                                           rq[:, 4 * k:4 * k + 4, :].rearrange("p j h -> p (j h)").unsqueeze(2)
                                           .broadcast_to([P, 4 * H, DH]), ALU.mult)
                last.then_inc(s_o_sb, 1)
                dve.wait_ge(s_wo_ps, b + 1)
                for k in range(2):
                    last = v.tensor_tensor(qk[:, 0, 4 * k:4 * k + 4, :], lb3(2 + k), tmp[:, 0, 4 * k:4 * k + 4, :], ALU.add)
                link(last)
                statistics(qk[:, 0], b * J, J, EPS_ATTN_OUT)
                dve.wait_ge(s_yn, b + 1)
                link(v.tensor_tensor(tmp[:, 1], tmp[:, 1], gammab, ALU.mult))
                v.tensor_tensor(xb(b), xb(b), tmp[:, 1], ALU.add).then_inc(s_x2, 1)
                dve.wait_ge(s_x2, b + 1)

            def finish(b):
                combine(B + b)

            def fold_biases():
                dve.wait_ge(s_brow_in, 16 * 5)
                dve.wait_ge(s_bf_ps, 1)
                v.tensor_tensor(bvcol[:], LB[3][:, 2 * D:2 * D + 1], bcol[:, 3:4], ALU.add)
                v.tensor_tensor(bfold[:], LB[3][:, 0:2 * D].rearrange("p (i d) -> p i d", i=2), brow[:, 0:2, :], ALU.add)\
                    .then_inc(s_bf_sb, 1)

            setup()
            for job in PLAN:
                if job[0] == "R":
                    route(job[1], job[2])
                    if job[1] == 0:
                        fold_biases()
                elif job[0] == "C":
                    ffn(job[1])
                elif job[0] == "M":
                    attend(job[1])
                else:
                    finish(job[1])


def kernel(**inputs):
    import numpy as _np
    import concourse.bacc as _bacc
    from concourse import mybir as _mybir
    from concourse.bass_utils import run_bass_kernel_spmd as _run

    names = ["L0_attn_" + n for n in ("x", "Wq", "bq", "Wk", "bk", "Wv", "bv", "Wq2", "bq2", "Wk2", "bk2", "Wv2", "bv2",
                                      "Wo", "bo", "gamma", "beta")]
    names += ["L0_ffn_" + n for n in ("gate_w", "w1", "b1", "w2", "b2")]
    nc = _bacc.Bacc("TRN2", target_bir_lowering=False, num_devices=1)
    arrays, args = {}, []
    for name in names:
        a = _np.ascontiguousarray(inputs[name])
        arrays[f"in_{name}_dram"] = a
        args.append(nc.dram_tensor(f"in_{name}_dram", a.shape, _mybir.dt.from_np(a.dtype), kind="ExternalInput").ap())
    args.append(nc.dram_tensor("out_dram", (B, L, D), _mybir.dt.float32, kind="ExternalOutput").ap())
    macaron(nc, *args)
    r = _run(nc, [arrays], core_ids=[0])
    return r.results[0]["out_dram"]
```

```python
from contextlib import ExitStack

import concourse.bass as bass
from concourse import mybir

P = 128
B, L, D = 4, 1024, 128
E, F, TOPK = 8, 512, 2
H, DH = 16, 8
J = L // P
NC = TOPK * J
FC = F // P
NT = (L * TOPK - E) // P + E
SLOTS = NT * P
NTP = NT + 2
SEL = 256.0
XS = 16.0
EPS_FFN, EPS_ATTN_OUT, EPS_QK = 1e-5, 1e-3, 1e-6

ALU = mybir.AluOpType
ACT = mybir.ActivationFunctionType
AX = mybir.AxisListType.X
F32, F16, I32 = mybir.dt.float32, mybir.dt.float16, mybir.dt.int32
U32, U8, BF16 = mybir.dt.uint32, mybir.dt.uint8, mybir.dt.bfloat16
HALF = 2
RMAX = bass.bass_isa.ReduceOp.max



def macaron(nc, A_x, Wq, bq, Wk, bk, Wv, bv, Wq2, bq2, Wk2, bk2, Wv2, bv2, Wo, bo, gamma, beta,
            gate_w, w1, b1, w2, b2, out):
    with ExitStack() as ctx:
        def sb(name, shape, dt=F32):
            return ctx.enter_context(nc.sbuf_tensor(name, shape, dt))

        def ps(name, shape, dt=F32):
            return ctx.enter_context(nc.psum_tensor(name, shape, dt))

        def sem(name):
            return ctx.enter_context(nc.semaphore(name))

        s_w1_in = sem("w1_in")
        s_w2_in = sem("w2_in")
        s_b1_in = sem("b1_in")
        s_b2_in = sem("b2_in")
        s_gate_in = sem("gate_in")
        s_wqkv_in = sem("wqkv_in")
        s_wqkv2_in = sem("wqkv2_in")
        s_wo_in = sem("wo_in")
        s_bcol_in = sem("bcol_in")
        s_brow_in = sem("brow_in")
        s_zero_set = sem("zero_set")
        s_consts = sem("consts")
        s_dve_order = sem("dve_order")
        s_absmax = sem("absmax")
        s_absmax_row = sem("absmax_row")
        s_largest = sem("largest")
        s_largest_all = sem("largest_all")
        s_scales = sem("scales")
        s_w1_hi = sem("w1_hi")
        s_w2_hi = sem("w2_hi")
        s_w1_lo = sem("w1_lo")
        s_w2_lo = sem("w2_lo")
        s_b1_hi = sem("b1_hi")
        s_b1_lo = sem("b1_lo")
        s_b2_hi = sem("b2_hi")
        s_b2_lo = sem("b2_lo")
        s_sel16 = sem("sel16")
        s_b2_zero = sem("b2_zero")
        s_gate_ps = sem("gate_ps")
        s_gate_sb = sem("gate_sb")
        s_wT_ps = sem("wT_ps")
        s_wT_sb = sem("wT_sb")
        s_wf_ps = sem("wf_ps")
        s_wf_sb = sem("wf_sb")
        s_bf_ps = sem("bf_ps")
        s_bf_sb = sem("bf_sb")
        s_route_stats = sem("route_stats")
        s_attn_stats = sem("attn_stats")
        s_xn = sem("xn")
        s_xhi = sem("xhi")
        s_xs_rows = sem("xs_rows")
        s_xnT_ps = sem("xnT_ps")
        s_xnT_sb = sem("xnT_sb")
        s_logits = sem("logits")
        s_zs = sem("zs")
        s_ez = sem("ez")
        s_e2 = sem("e2")
        s_z2 = sem("z2")
        s_tile_counts = sem("tile_counts")
        s_prefix = sem("prefix")
        s_eids = sem("eids")
        s_gates = sem("gates")
        s_gT_ps = sem("gT_ps")
        s_gT_sb = sem("gT_sb")
        s_b2_ps = sem("b2_ps")
        s_b2_added = sem("b2_added")
        s_pos = sem("pos")
        s_xT_ps = sem("xT_ps")
        s_xT_sb = sem("xT_sb")
        s_h_ps = sem("h_ps")
        s_h_hi = sem("h_hi")
        s_h_lo = sem("h_lo")
        s_y_ps = sem("y_ps")
        s_y_sb = sem("y_sb")
        s_y_stored = sem("y_stored")
        s_comb = sem("comb")
        s_xa = sem("xa")
        s_xaT_ps = sem("xaT_ps")
        s_xaT_sb = sem("xaT_sb")
        s_v_ps = sem("v_ps")
        s_v_sb = sem("v_sb")
        s_q_ps = sem("q_ps")
        s_k_ps = sem("k_ps")
        s_eq = sem("eq")
        s_ek = sem("ek")
        s_fq = sem("fq")
        s_fk = sem("fk")
        s_s_ps = sem("s_ps")
        s_s_sb = sem("s_sb")
        s_o_ps = sem("o_ps")
        s_o_sb = sem("o_sb")
        s_oT_ps = sem("oT_ps")
        s_oT_sb = sem("oT_sb")
        s_res_ps = sem("res_ps")
        s_wo_ps = sem("wo_ps")
        s_yn = sem("yn")
        s_x2 = sem("x2")
        s_out_stored = sem("out_stored")

        s_xn = [sem("xn_even"), sem("xn_odd")]
        s_xnT_sb = [sem("xnT_sb_even"), sem("xnT_sb_odd")]
        x_in = [sem(f"x_in{b}") for b in range(B)]
        xs_zeroed = [sem(f"xs_zeroed{i}") for i in range(2)]
        scattered = [sem(f"scattered{i}") for i in range(2)]
        gathered = [[sem(f"gathered{i}{k}") for k in range(TOPK)] for i in range(2)]
        slots_in = [[sem(f"slots_in{i}{k}") for k in "abc"] for i in range(2)]

        xs_dram = [nc.dram_tensor(f"xs_dram{i}", [SLOTS, 2 * D], F16).ap() for i in range(2)]
        y_dram = [nc.dram_tensor(f"y_dram{b}", [SLOTS, D], F32).ap() for b in range(B)]

        x = sb("x", [P, B * J, D])
        w1_bytes = sb("w1_bytes", [P, E * 2 * F * HALF], U8)
        w2_bytes = sb("w2_bytes", [P, E * 2 * F * HALF], U8)
        w1s, w2s = w1_bytes[:].bitcast(F16), w2_bytes[:].bitcast(F16)
        wraw = sb("wraw", [P, E * F])
        wraw2 = sb("wraw2", [P, E * F])
        b1raw = sb("b1raw", [40, F])
        b1s = sb("b1s", [P, F], F16)
        b1h = sb("b1h", [40, F], F16)
        sel_bytes = sb("sel_bytes", [P, E * P * HALF], U8)
        sel = sel_bytes[:].bitcast(F16)
        b2raw = sb("b2raw", [40, D])
        b2s = sb("b2s", [P, D], F16)
        b2h = sb("b2h", [40, D], F16)
        pick16 = sb("pick16", [P, 40], F16)
        gate_sb = sb("gate_sb", [E, D])
        gateT = sb("gateT", [P, E])
        wq_sb = sb("wq_sb", [P, 3, D])
        wqT = sb("wqT", [P, 3, D])
        wq2_sb = sb("wq2_sb", [P, 3, D])
        wf = sb("wf", [P, 3, D])
        wo_sb = sb("wo_sb", [P, D])
        bcol = sb("bcol", [P, 4])
        brow = sb("brow", [P, 5, D])
        bvcol = sb("bvcol", [P, 1])
        rowpart = sb("rowpart", [P, 3, D], BF16)
        rowrest = sb("rowrest", [P, 3, D])
        rows3 = sb("rows3", [P, 3, D], BF16)
        ones3 = sb("ones3", [P, P], BF16)
        amax = sb("amax", [P, 4])
        scl = sb("scl", [P, 16])
        ident = sb("ident", [P, P])
        ident16 = sb("ident16", [P, P], F16)
        tri = sb("tri", [P, P])
        ones = sb("ones", [P, P])
        headmask = sb("headmask", [P, P])
        rev = sb("rev", [P, E])
        thr = sb("thr", [P, J])
        tnum = sb("tnum", [P, NTP])
        keep = sb("keep", [P, B * E * NC])
        zeros = sb("zeros", [P, 2 * D], F16)
        minus1 = sb("minus1", [P, 1])
        amax_row = sb("amax_row", [4, 1])

        st = sb("st", [P, B * J, 6])
        lnw = sb("lnw", [P, 8, B * J])
        lni = sb("lni", [P, B * J], I32)
        xn = sb("xn", [P, 2, J, D])
        xnT_even = sb("xnT_even", [P, L])
        xs = sb("xs", [P, B * J, 2 * D], F16)
        zl = sb("zl", [P, 4, B * J, E])
        small = sb("small", [P, 8, B * J])
        masks = sb("masks", [P, B, E, NC])
        incl = sb("incl", [P, B, E, NC])
        mpos = sb("mpos", [P, B, E, NC])
        cnt = sb("cnt", [P, 6, B, E])
        cmp = sb("cmp", [P, B, E, J])
        cmpt = sb("cmpt", [1, B, NTP, E])
        eidf = sb("eidf", [1, B, NTP])
        eidw = sb("eidw", [1, B, NT])
        eids = sb("eids", [1, 2 * B * NT], I32)
        posf = sb("posf", [P, 3, B, NC], I32)
        posr = sb("posr", [P, B, NC])
        rows = sb("rows", [P, 2 * B, NC], I32)
        g12 = sb("g12", [P, 2 * B, NC])
        keep8 = sb("keep8", [P, B, E])

        xsort = [sb(f"xsort{i}", [P, NT, 2 * D], F16) for i in range(2)]
        xT = sb("xT", [P, 2, 2 * P], F16)
        hh = sb("hh", [P, 2, F], F16)
        hl = sb("hl", [P, 2, F], F16)
        yall = sb("yall", [P, NT, D])
        yg = [wraw2[:, 0:NC * D].rearrange("p (c d) -> p c d", c=NC), sb("yg1", [P, NC, D])[:]]
        sbd = sb("sbd", [P, 2, P])
        qks = sb("qks", [P, 2, J, H])
        rq = sb("rq", [P, 2, J, H])

        LB = [ps(f"LB{i}", [P, 512]) for i in range(4)]
        xTp = ps("xTp", [P, 1024], F16)
        hp = [ps(f"hp{i}", [P, 512]) for i in range(2)]
        yp = ps("yp", [P, 512])

        class Attention:
            def __init__(self, wide, columns, banks, m):
                self.qk = wide[0].rearrange("p (i j d) -> p i j d", i=2, j=J)
                self.tmp = wide[1].rearrange("p (i j d) -> p i j d", i=2, j=J)
                self.xaT, self.vT = columns[:, 0:L], columns[:, L:2 * L]
                self.bank = banks
                self.exps = xn[:, m]
                self.sbd, self.qks, self.rq = sbd[:, m], qks[:, m], rq[:, m]

            def tiles(self, i):
                return self.bank[i].rearrange("p (j d) -> p j d", j=4)

        xs_wide = xs[:].rearrange("p j c -> p (j c)").bitcast(F32)
        half = B * J * D // 2
        AT = [Attention((wraw2[:, NC * D:], wraw[:, 2 * L:]), wraw[:, 0:2 * L], [LB[i][:] for i in range(4)], 0),
              Attention((xs_wide[:, 0:half], xs_wide[:, half:]), yall[:].rearrange("p t d -> p (t d)")[:, 0:2 * L],
                        [hp[0][:], hp[1][:], yp[:], xTp[:].bitcast(F32)], 1)]

        xnT = [xnT_even[:], AT[1].xaT]

        def xb(b):
            return x[:, b * J:(b + 1) * J, :]

        PLAN = [("R", 0, [0, 1, 2, 3]), ("W",), ("C", 0), ("C", 1), ("C", 2), ("M", [0, 1]), ("R", 1, [0, 1]),
                ("C", 3), ("C", 4), ("M", [2, 3]), ("R", 1, [2, 3]), ("C", 5), ("F", 0), ("C", 6), ("F", 1), ("C", 7),
                ("F", 2), ("F", 3)]
        SPLIT = [(0, 5), (5, 13), (13, NT)]

        def r_index(f, bs):
            return 0 if f == 0 else 1 + bs[0] // 2

        def stored_before(bs):
            return 3 if bs[0] == 0 else 5

        def steps(engine, first, two_steps, step):
            first()
            step(0, 0)
            with engine.Fori(1, NT - 3, 2) as t:
                two_steps(t)
            two_steps(NT - 2)

        def beyond(t):
            return isinstance(t, int) and t >= NT

        block = ctx.enter_context(nc.Block())

        @block.sync
        def _(sp):
            def load_x(b):
                sp.dma_start(xb(b), A_x[b].rearrange("(p j) h -> p j h", j=J)).then_inc(x_in[b], 16)

            for b in range(B):
                load_x(b)
            sp.dma_start(gate_sb[:], gate_w).then_inc(s_gate_in, 16)
            sp.dma_start(wraw[:].rearrange("p (e f) -> p e f", e=E), w1.rearrange("e p f -> p e f")).then_inc(s_w1_in, 16)
            sp.dma_start(wraw2[:].rearrange("p (e c d) -> p e c d", e=E, c=FC),
                         w2.rearrange("e (c p) d -> p e c d", p=P)).then_inc(s_w2_in, 16)
            for r in (0, 32):
                sp.dma_start(b1raw[r:r + E, :], b1).then_inc(s_b1_in, 16)
                sp.dma_start(b2raw[r:r + E, :], b2).then_inc(s_b2_in, 16)
            sp.wait_ge(s_zero_set, 1)
            for i in range(2):
                sp.dma_start(xs_dram[i].rearrange("(p t) c -> p t c", t=NT), zeros[:].unsqueeze(1).broadcast_to([P, NT, 2 * D]))\
                    .then_inc(xs_zeroed[i], 16)
            for i, w in enumerate((Wq, Wk, Wv)):
                sp.dma_start(wq_sb[:, i, :], w).then_inc(s_wqkv_in, 16)
            for i, w in enumerate((Wq2, Wk2, Wv2)):
                sp.dma_start(wq2_sb[:, i, :], w).then_inc(s_wqkv2_in, 16)
            for i, v in enumerate((bq, bk, bv, bv2)):
                sp.dma_start(bcol[:, i:i + 1], v.rearrange("(p a) -> p a", a=1)).then_inc(s_bcol_in, 16)
            for i, v in enumerate((bq2, bk2, bo, gamma, beta)):
                sp.dma_start(brow[:, i, :], v.rearrange("(a d) -> a d", a=1).broadcast_to([P, D])).then_inc(s_brow_in, 16)
            sp.dma_start(wo_sb[:], Wo).then_inc(s_wo_in, 16)

            def load_slots(i):
                sp.wait_ge(scattered[i % 2], 16 * NC * (i // 2 + 1))
                if i >= 2:
                    sp.wait_ge(s_xT_ps, NT * (i - 1))
                src = xs_dram[i % 2].rearrange("(p t) c -> p t c", t=NT)
                for (lo, hi), landed in zip(SPLIT, slots_in[i % 2]):
                    sp.dma_start(xsort[i % 2][:, lo:hi, :], src[:, lo:hi, :]).then_inc(landed, 16)

            def store_slots(i):
                dst = y_dram[i % B].rearrange("(p t) c -> p t c", t=NT)
                for lo, hi in SPLIT:
                    sp.wait_ge(s_y_sb, NT * i + hi)
                    sp.dma_start(dst[:, lo:hi, :], yall[:, lo:hi, :]).then_inc(s_y_stored, 16)

            load_slots(0)
            load_slots(1)
            for i in range(2 * B):
                store_slots(i)
                if i + 2 < 2 * B:
                    load_slots(i + 2)
            for b in range(B):
                sp.wait_ge(s_comb, B + b + 1)
                sp.dma_start(out[b].rearrange("(p j) h -> p j h", j=J), xb(b)).then_inc(s_out_stored, 16)
            sp.wait_ge(s_out_stored, 16 * B)

        @block.gpsimd
        def _(pool):
            g = nc.gpsimd
            n = 0

            def order(ins):
                nonlocal n
                n += 1
                ins.then_inc(s_consts, 1)
                pool.wait_ge(s_consts, n)

            order(g.memset(ones[:], 1.0))
            order(g.affine_select(ident[:], ones[:], [[-1, P]], ALU.is_equal, 0.0, base=0, channel_multiplier=1))
            order(g.affine_select(tri[:], ones[:], [[1, P]], ALU.is_gt, 0.0, base=0, channel_multiplier=-1))
            hm = headmask[:].rearrange("p (h e) -> p h e", e=DH)
            order(g.affine_select(hm, ones[:].rearrange("p (h e) -> p h e", e=DH), [[-DH, H], [0, DH]], ALU.is_ge, 0.0,
                                  base=0, channel_multiplier=1))
            order(g.affine_select(hm, hm, [[DH, H], [0, DH]], ALU.is_ge, 0.0, base=DH - 1, channel_multiplier=-1))
            order(g.iota(rev[:], [[-1, E]], base=E, channel_multiplier=0, allow_small_or_imprecise_dtypes=True))
            order(g.iota(thr[:], [[P, J]], base=0, channel_multiplier=0, allow_small_or_imprecise_dtypes=True))
            order(g.iota(tnum[:], [[1, NTP]], base=0, channel_multiplier=0, allow_small_or_imprecise_dtypes=True))
            order(g.memset(keep[:], 1.0))
            order(g.memset(keep[:].rearrange("p (g c) -> p g c", c=NC)[:, :, 0:1], 0.0))
            order(g.memset(keep8[:], 1.0))
            order(g.memset(keep8[:, :, 0:1], 0.0))
            def scatter(i):
                b = i % B
                pool.wait_ge(s_pos, i + 1)
                pool.wait_ge(s_xs_rows, i + 1)
                if i < 2:
                    pool.wait_ge(xs_zeroed[i], 16)
                else:
                    for landed in slots_in[i % 2]:
                        pool.wait_ge(landed, 16 * (i // 2))
                for c in range(NC):
                    g.indirect_dma_start(
                        out=xs_dram[i % 2], out_offset=bass.IndirectOffsetOnAxis(ap=rows[:, i, c:c + 1], axis=0),
                        in_=xs[:, b * J + c % J, :], in_offset=None).then_inc(scattered[i % 2], 16)

            def gather(i):
                pool.wait_ge(s_y_stored, 16 * len(SPLIT) * (i + 1))
                if i >= 2:
                    pool.wait_ge(s_comb, i - 1)
                for c in range(NC):
                    g.indirect_dma_start(
                        out=yg[i % 2][:, c, :], out_offset=None, in_=y_dram[i % B],
                        in_offset=bass.IndirectOffsetOnAxis(ap=rows[:, i, c:c + 1], axis=0))\
                        .then_inc(gathered[i % 2][c // J], 16)

            for i in range(B):
                scatter(i)
            for i in range(3):
                gather(i)
            scatter(4)
            scatter(5)
            gather(3)
            gather(4)
            scatter(6)
            scatter(7)
            for i in range(5, 2 * B):
                gather(i)

        @block.tensor
        def _(pe):
            mm, tr = nc.tensor.matmul, nc.tensor.transpose
            word = pe.alloc_register("experts_of_tiles")

            def setup():
                pe.wait_ge(s_consts, 12)
                pe.wait_ge(s_gate_in, 16)
                tr(LB[0][:, 0:E], gate_sb[:], ident[0:E, 0:E]).then_inc(s_gate_ps, 1)

            def fold():
                pe.wait_ge(s_wqkv_in, 16 * 3)
                for i in range(3):
                    last = tr(LB[1][:, i * D:(i + 1) * D], wq_sb[:, i, :], ident[:])
                last.then_inc(s_wT_ps, 1)
                pe.wait_ge(s_wT_sb, 1)
                pe.wait_ge(s_wqkv2_in, 16 * 3)
                for i in range(3):
                    last = mm(LB[1][:, i * D:(i + 1) * D], wqT[:, i, :], wq2_sb[:, i, :], start=True, stop=True)
                last.then_inc(s_wf_ps, 1)

            def fold_biases():
                pe.wait_ge(s_bcol_in, 16 * 4)
                for i in range(2):
                    mm(LB[3][:, i * D:(i + 1) * D], bcol[:, i:i + 1].broadcast_to([P, P]), wq2_sb[:, i, :], start=True, stop=True)
                mm(LB[3][:, 2 * D:2 * D + 1], wq2_sb[:, 2, :], bcol[:, 2:3], start=True, stop=True).then_inc(s_bf_ps, 1)

            def largest():
                pe.wait_ge(s_absmax, 1)
                pe.wait_ge(s_zs, 1)
                tr(LB[2][0:4, 0:P], amax[:], ident[:]).then_inc(s_absmax_row, 1)
                pe.wait_ge(s_largest, 1)
                mm(LB[2][:, 0:4], amax_row[:].broadcast_to([4, P]), ident[0:4, 0:4], start=True, stop=True).then_inc(s_largest_all, 1)

            def weights_ready():
                fold()
                largest()
                pe.wait_ge(s_eids, 1)
                fold_biases()

            def route(f, bs):
                if f:
                    pe.wait_ge(s_x2, bs[-1] + 1)
                else:
                    pe.wait_ge(s_gate_sb, 1)
                for b0 in bs[::2]:
                    for p in range(2):
                        i = f * B + b0 + p
                        pe.wait_ge(s_xn[p], i // 2 + 1)
                        if i >= 2:
                            pe.wait_ge(s_xnT_sb[p], i // 2)
                        for j in range(J):
                            last = tr(AT[p].bank[j // 4][:, (j % 4) * P:(j % 4 + 1) * P], xn[:, p, j, :], ident[:])
                        last.then_inc(s_xnT_ps, 1)
                    for p in range(2):
                        b = b0 + p
                        pe.wait_ge(s_xnT_sb[p], (f * B + b) // 2 + 1)
                        for j in range(J):
                            last = mm(LB[2][:, (b * J + j) * E:(b * J + j + 1) * E], xnT[p][:, j * P:(j + 1) * P], gateT[:],
                                      start=True, stop=True)
                        last.then_inc(s_logits, 1)
                q = r_index(f, bs)
                pe.wait_ge(s_tile_counts, q + 1)
                for k, lhs in enumerate((tri, ones)):
                    for b in bs:
                        last = mm(LB[3][:, (k * B + b) * E:(k * B + b + 1) * E], lhs[:], incl[:, b, :, NC - 1],
                                  start=True, stop=True)
                last.then_inc(s_prefix, 1)

            def ffn(i):
                g0 = i * NT
                slots = xsort[i % 2][:].rearrange("p t c -> p (t c)")

                def fetch(t):
                    pe.reg_load(word, eids[0:1, bass.ds(t + g0, 1)])

                def experts():
                    w = pe.snap(word)
                    return [pe.snap(q % E) for q in (w, w // E, w // (E * E))]

                def slot_rows(t):
                    return [slots[:, bass.ds(t * (2 * D) + k * D, D)] for k in range(2)]

                def weights(table, e):
                    pick = sel_bytes[:, bass.ds(e * (P * HALF), P * HALF)].bitcast(F16)
                    return pick, [[table[:, bass.ds(e * (2 * F * HALF) + (part * F + c * P) * HALF, P * HALF)].bitcast(F16)
                                   for part in range(2)] for c in range(FC)]

                def address(aps, stationary):
                    for ap in aps:
                        pe.lower_ap(ap, for_matmul_weights=stationary)

                def turn(t, src):
                    for k in range(2):
                        last = tr(xTp[:, k * P:(k + 1) * P], src[k], ident16[:])
                    last.then_inc(s_xT_ps, 1)

                def up(t, p, pick, w, src):
                    pe.wait_ge(s_xT_sb, t + (g0 + 1))
                    hi, lo = xT[:, p, 0:P], xT[:, p, P:2 * P]
                    for c, (wh, wl) in enumerate(w):
                        o = hp[p][:, c * P:(c + 1) * P]
                        mm(o, b1s[:, c * P:(c + 1) * P], pick, start=True, stop=False)
                        mm(o, wh, hi, start=False, stop=False)
                        mm(o, wh, lo, start=False, stop=False)
                        last = mm(o, wl, hi, start=False, stop=True)
                        if c == 0 and not beyond(t + 1):
                            turn(t + 1, src)
                    last.then_inc(s_h_ps, 1)

                def down(t, p, pick, w):
                    if isinstance(t, int) and t == 0:
                        pe.wait_ge(s_h_hi, g0 + 1)
                    else:
                        pe.wait_ge(s_y_sb, t + g0)
                    for c, (wh, wl) in enumerate(w):
                        for part in (wh, wl):
                            mm(yp[:, 0:D], hh[:, p, c * P:(c + 1) * P], part, start=(c == 0 and part is wh), stop=False)
                    mm(yp[:, 0:D], pick, b2s[:], start=False, stop=False)
                    pe.wait_ge(s_h_lo, t + (g0 + 1))
                    for c, (wh, wl) in enumerate(w):
                        last = mm(yp[:, 0:D], hl[:, p, c * P:(c + 1) * P], wh, start=False, stop=(c == FC - 1))
                    last.then_inc(s_y_ps, 1)

                def one_step(t, p, e_now, e_next):
                    if not beyond(t + 1):
                        pick, w1e = weights(w1_bytes, e_next)
                        address([part for chunk in w1e for part in chunk], True)
                        address([pick], False)
                    src = slot_rows(t + 2) if not beyond(t + 2) else []
                    address(src, True)
                    if not beyond(t + 1):
                        up(t + 1, 1 - p, pick, w1e, src)
                    pick, w2e = weights(w2_bytes, e_now)
                    address([part for chunk in w2e for part in chunk], False)
                    address([pick], True)
                    down(t, p, pick, w2e)

                def step(t, p):
                    e = experts()
                    fetch(t + 1)
                    one_step(t, p, e[0], e[1])

                def two_steps(t):
                    e = experts()
                    one_step(t, 1, e[0], e[1])
                    if not beyond(t + 2):
                        fetch(t + 2)
                    one_step(t + 1, 0, e[1], e[2])

                def first():
                    pe.wait_ge(s_eids, 1 if i < B else i // 2)
                    if i == 0:
                        pe.wait_ge(s_w1_hi, 1)
                        pe.wait_ge(s_w1_lo, 1)
                        pe.wait_ge(s_b1_lo, 1)
                        pe.wait_ge(s_sel16, 1)
                    for landed in slots_in[i % 2]:
                        pe.wait_ge(landed, 16 * (i // 2 + 1))
                    turn(0, slot_rows(0))
                    fetch(0)
                    up(0, 0, *weights(w1_bytes, experts()[0]), slot_rows(1))
                    if i == 0:
                        pe.wait_ge(s_w2_hi, 1)
                        pe.wait_ge(s_b2_lo, 1)
                        pe.wait_ge(s_w2_lo, 1)

                steps(pe, first, two_steps, step)

            def attend(bs):
                if bs[0] == 0:
                    pe.wait_ge(s_wo_in, 16)

                def tile(t, j):
                    return t.bank[j // 4][:, (j % 4) * P:(j % 4 + 1) * P]

                def row(r):
                    return r.unsqueeze(1).broadcast_to([P, 4, D])

                def columns(b, t):
                    pe.wait_ge(s_xa, b + 1)
                    for j in range(J):
                        last = tr(tile(t, j), t.tmp[:, 0, j, :], ident[:])
                    last.then_inc(s_xaT_ps, 1)

                def keys_and_queries(b, t):
                    pe.wait_ge(s_xaT_sb, b + 1)
                    for i, bank, done in ((1, 2, s_k_ps), (0, 0, s_q_ps)):
                        for k in range(2):
                            mm(t.bank[bank + k], ones3[:], row(rows3[:, i, :]), start=True, stop=False)
                        for j in range(J):
                            last = mm(tile(t, 4 * bank + j), t.xaT[:, j * P:(j + 1) * P], wf[:, i, :], start=False, stop=(j % 4 == 3))
                        last.then_inc(done, 1)

                def states_and_values(b, t):
                    pe.wait_ge(s_fk, b + 1)
                    pe.wait_ge(s_fq, b + 1)
                    for j in range(J):
                        last = mm(t.bank[2][:, 0:P], t.qk[:, 1, j, :], t.qk[:, 0, j, :], start=(j == 0), stop=(j == J - 1))
                    last.then_inc(s_s_ps, 1)
                    for k in range(2):
                        last = mm(t.bank[k], wf[:, 2, :], t.xaT[:, k * 512:(k + 1) * 512], start=True, stop=True)
                    last.then_inc(s_v_ps, 1)

                def heads(b, t):
                    pe.wait_ge(s_s_sb, b + 1)
                    pe.wait_ge(s_v_sb, b + 1)
                    for j in range(J):
                        last = mm(tile(t, j), t.vT[:, j * P:(j + 1) * P], t.sbd, start=True, stop=True)
                    last.then_inc(s_o_ps, 1)

                def residual(b, t):
                    for k in range(2):
                        mm(t.bank[2 + k], ones3[:], row(rows3[:, 2, :]), start=True, stop=False)
                    for j in range(J):
                        last = mm(tile(t, J + j), t.xaT[:, j * P:(j + 1) * P], ident[:], start=False, stop=False)
                    last.then_inc(s_res_ps, 1)

                def head_columns(b, t):
                    pe.wait_ge(s_o_sb, b + 1)
                    for j in range(J):
                        last = tr(tile(t, j), t.tmp[:, 1, j, :], ident[:])
                    last.then_inc(s_oT_ps, 1)

                def output(b, t):
                    pe.wait_ge(s_oT_sb, b + 1)
                    for j in range(J):
                        last = mm(tile(t, J + j), t.xaT[:, j * P:(j + 1) * P], wo_sb[:], start=False, stop=(j % 4 == 3))
                    last.then_inc(s_wo_ps, 1)

                first, second = [(b, AT[b % 2]) for b in bs]
                for b in (first, second):
                    columns(*b)
                    keys_and_queries(*b)
                for b in (first, second):
                    states_and_values(*b)
                heads(*first)
                heads(*second)
                for b in (first, second):
                    residual(*b)
                    head_columns(*b)
                output(*first)
                output(*second)

            setup()
            for job in PLAN:
                if job[0] == "R":
                    route(job[1], job[2])
                elif job[0] == "W":
                    weights_ready()
                elif job[0] == "C":
                    ffn(job[1])
                elif job[0] == "M":
                    attend(job[1])

        @block.scalar
        def _(act):
            a = nc.scalar.activation

            def setup():
                act.wait_ge(s_gate_ps, 1)
                a(gateT[:], LB[0][:, 0:E], ACT.Copy).then_inc(s_gate_sb, 1)

            def fold():
                act.wait_ge(s_wT_ps, 1)
                a(wqT[:].rearrange("p i d -> p (i d)"), LB[1][:, 0:3 * D], ACT.Copy).then_inc(s_wT_sb, 1)
                act.wait_ge(s_wf_ps, 1)
                a(wf[:].rearrange("p i d -> p (i d)"), LB[1][:, 0:3 * D], ACT.Copy).then_inc(s_wf_sb, 1)

            def split_weights():
                act.wait_ge(s_scales, 1)
                a(w1s.rearrange("p (e k f) -> p e k f", e=E, k=2)[:, :, 0, :], wraw[:].rearrange("p (e f) -> p e f", e=E),
                  ACT.Copy, scale=scl[:, 0:1]).then_inc(s_w1_hi, 1)
                a(b1s[0:E, :], b1raw[0:E, :], ACT.Copy, scale=scl[0:E, 6:7])
                a(b1h[32:40, :], b1raw[32:40, :], ACT.Copy, scale=scl[32:40, 6:7]).then_inc(s_b1_hi, 1)
                a(b2s[0:E, :], b2raw[0:E, :], ACT.Copy, scale=scl[0:E, 12:13])
                a(b2h[32:40, :], b2raw[32:40, :], ACT.Copy, scale=scl[32:40, 12:13]).then_inc(s_b2_hi, 1)
                a(w2s.rearrange("p (e k f) -> p e k f", e=E, k=2)[:, :, 0, :], wraw2[:].rearrange("p (e f) -> p e f", e=E),
                  ACT.Copy, scale=scl[:, 1:2]).then_inc(s_w2_hi, 1)

            def normalise(dst, src, lo, last_sem, m=J):
                for j in range(m):
                    last = a(dst[:, j, :], src[:, j, :], ACT.Identity, scale=lnw[:, 5, lo + j:lo + j + 1],
                             bias=lnw[:, 6, lo + j:lo + j + 1])
                if last_sem is not None:
                    last.then_inc(last_sem, 1)

            def evacuate(dst, banks, sem):
                for k in range(2):
                    last = a(dst[:, k * 512:(k + 1) * 512], banks[k][:, :], ACT.Copy)
                last.then_inc(sem, 1)

            def route(f, bs):
                q = r_index(f, bs)
                act.wait_ge(s_route_stats, q + 1)
                for b in bs[::2]:
                    i = f * B + b
                    if i >= 2:
                        act.wait_ge(s_xnT_ps, i - 1)
                        act.wait_ge(s_xs_rows, i - 1)
                    normalise(xn[:, 0], xb(b), b * J, s_xn[0])
                    high_rows(f, b)
                    act.wait_ge(s_xnT_ps, i + 1)
                    if i >= 2:
                        act.wait_ge(s_logits, i - 1)
                    evacuate(xnT[0], AT[0].bank, s_xnT_sb[0])
                    high_rows(f, b + 1)
                act.wait_ge(s_zs, q + 1)
                lo, hi = bs[0] * J, (bs[-1] + 1) * J
                a(zl[:, 1, lo:hi, :], zl[:, 0, lo:hi, :], ACT.Exp).then_inc(s_ez, 1)
                act.wait_ge(s_z2, q + 1)
                a(small[:, 3, lo:hi], small[:, 2, lo:hi], ACT.Exp).then_inc(s_e2, 1)

            def high_rows(f, b):
                act.wait_ge(s_xn[b % 2], (f * B + b) // 2 + 1)
                if f:
                    act.wait_ge(scattered[b % 2], 16 * NC * (b // 2 + 1))
                a(xs[:, b * J:(b + 1) * J, 0:D], xn[:, b % 2], ACT.Copy, scale=XS).then_inc(s_xhi, 1)

            def ffn(i):
                g0 = i * NT
                results = yall[:].rearrange("p t c -> p (t c)")

                def high(t, p):
                    act.wait_ge(s_h_ps, t + (g0 + 1))
                    a(hh[:, p, :], hp[p][:], ACT.Relu).then_inc(s_h_hi, 1)

                def result(t):
                    act.wait_ge(s_y_ps, t + (g0 + 1))
                    if isinstance(t, int) and t == 0 and i:
                        act.wait_ge(s_y_stored, 16 * len(SPLIT) * i)
                    a(results[:, bass.ds(t * D, D)], yp[:, 0:D], ACT.Copy, scale=scl[:, 3:4]).then_inc(s_y_sb, 1)

                def step(t, p):
                    if not beyond(t + 1):
                        high(t + 1, 1 - p)
                    result(t)

                def two_steps(t):
                    step(t, 1)
                    step(t + 1, 0)

                steps(act, lambda: high(0, 0), two_steps, step)

            def attend(bs):
                def inputs(b, t):
                    act.wait_ge(s_attn_stats, 2 * bs[0] + b % 2 + 1)
                    normalise(t.tmp[:, 0], xb(b), b * J, s_xa)

                def columns(b, t):
                    act.wait_ge(s_xaT_ps, b + 1)
                    if b % 2:
                        act.wait_ge(s_y_stored, 16 * len(SPLIT) * stored_before(bs))
                    evacuate(t.xaT, t.bank, s_xaT_sb)

                def exponentials(b, t, ready, bank, done):
                    act.wait_ge(ready, b + 1)
                    for k in range(2):
                        last = a(t.exps.rearrange("p j d -> p (j d)")[:, k * 512:(k + 1) * 512], t.bank[bank + k], ACT.Exp, bias=minus1[:])
                    last.then_inc(done, 1)

                def of_keys(b, t):
                    exponentials(b, t, s_k_ps, 2, s_ek)

                def of_queries(b, t):
                    act.wait_ge(s_fk, b + 1)
                    exponentials(b, t, s_q_ps, 0, s_eq)

                def values(b, t):
                    act.wait_ge(s_v_ps, b + 1)
                    for k in range(2):
                        last = a(t.vT[:, k * 512:(k + 1) * 512], t.bank[k], ACT.Identity, bias=bvcol[:])
                    last.then_inc(s_v_sb, 1)

                def head_columns(b, t):
                    act.wait_ge(s_oT_ps, b + 1)
                    act.wait_ge(s_res_ps, b + 1)
                    evacuate(t.xaT, t.bank, s_oT_sb)

                def outputs(b, t):
                    act.wait_ge(s_attn_stats, 2 * bs[0] + 2 + b % 2 + 1)
                    for k in range(2):
                        normalise(t.tmp[:, 1, 4 * k:4 * k + 4, :], t.tiles(2 + k), b * J + 4 * k, s_yn if k else None, 4)

                first, second = [(b, AT[b % 2]) for b in bs]
                inputs(*first)
                columns(*first)
                of_keys(*first)
                inputs(*second)
                of_queries(*first)
                columns(*second)
                of_keys(*second)
                of_queries(*second)
                for step in (values, head_columns, outputs):
                    step(*first)
                    step(*second)

            setup()
            for job in PLAN:
                if job[0] == "R":
                    route(job[1], job[2])
                elif job[0] == "W":
                    fold()
                    split_weights()
                elif job[0] == "C":
                    ffn(job[1])
                elif job[0] == "M":
                    if job[1][0] == 0:
                        act.wait_ge(s_bf_sb, 1)
                    attend(job[1])

        @block.vector
        def _(dve):
            v = nc.vector
            n = 0

            def link(ins):
                nonlocal n
                n += 1
                ins.then_inc(s_dve_order, 1)
                dve.wait_ge(s_dve_order, n)

            def setup():
                v.memset(zeros[:].bitcast(U32), 0).then_inc(s_zero_set, 1)
                v.memset(minus1[:], -1.0)
                v.memset(b1s[:].bitcast(U32), 0)
                v.memset(b2s[:].bitcast(U32), 0)
                v.memset(rows3[:].bitcast(U32), 0)
                link(v.memset(ones3[:], 1.0))
                dve.wait_ge(s_consts, 12)
                v.tensor_copy(ident16[:], ident[:])
                link(v.tensor_scalar(pick16[:], ident[:, 0:40], SEL, None, ALU.mult))
                v.tensor_tensor(sel.rearrange("p (e t) -> p e t", e=E), pick16[:, 0:E].unsqueeze(2).broadcast_to([P, E, P]),
                                pick16[:, 32:32 + E].unsqueeze(2).broadcast_to([P, E, P]), ALU.add).then_inc(s_sel16, 1)

            def power(src, dst, by):
                link(v.tensor_scalar(scl[:, src:src + 1], scl[:, src:src + 1], 1e-15, 1e15, ALU.max, ALU.min))
                bits = scl[:].bitcast(U32)
                link(v.tensor_scalar(bits[:, src:src + 1], bits[:, src:src + 1], 0x7F800000, 0x7F800000,
                                     ALU.bitwise_and, ALU.bitwise_xor))
                link(v.tensor_scalar(scl[:, dst:dst + 1], scl[:, src:src + 1], by, None, ALU.mult))

            def split_weights():
                link(v.memset(amax[:], 0.0))
                for k, (raw, landed, lanes) in enumerate(((wraw, s_w1_in, P), (b1raw, s_b1_in, E), (wraw2, s_w2_in, P), (b2raw, s_b2_in, E))):
                    dve.wait_ge(landed, 16 if lanes == P else 32)
                    last = v.tensor_reduce(amax[0:lanes, k:k + 1], raw[0:lanes, :], AX, ALU.max, apply_absolute_value=True)
                last.then_inc(s_absmax, 1)
                dve.wait_ge(s_absmax_row, 1)
                v.tensor_reduce(amax_row[:], LB[2][0:4, 0:P], AX, ALU.max).then_inc(s_largest, 1)
                dve.wait_ge(s_largest_all, 1)
                link(v.tensor_copy(scl[:, 8:12], LB[2][:, 0:4]))
                link(v.scalar_tensor_tensor(scl[:, 4:5], scl[:, 8:9], float(D), scl[:, 9:10], ALU.mult, ALU.max))
                power(4, 0, 2.0 ** 8)
                link(v.tensor_scalar(scl[:, 2:3], scl[:, 0:1], XS, None, ALU.mult))
                v.tensor_scalar(scl[:, 6:7], scl[:, 2:3], 1.0 / SEL, None, ALU.mult)
                link(v.scalar_tensor_tensor(scl[:, 5:6], scl[:, 2:3], 2.0 ** -10, scl[:, 11:12], ALU.mult, ALU.mult))
                link(v.tensor_tensor(scl[:, 5:6], scl[:, 5:6], scl[:, 10:11], ALU.max))
                power(5, 1, 2.0 ** 12)
                link(v.tensor_tensor(scl[:, 7:8], scl[:, 1:2], scl[:, 2:3], ALU.mult))
                v.reciprocal(scl[:, 3:4], scl[:, 7:8])
                v.tensor_scalar(scl[:, 12:13], scl[:, 7:8], 1.0 / SEL, None, ALU.mult).then_inc(s_scales, 1)

                def low(dst, raw, scale, high, done):
                    v.scalar_tensor_tensor(dst, raw, scale, high, ALU.mult, ALU.subtract).then_inc(done, 1)

                def by_expert(t, k):
                    return t.rearrange("p (e k f) -> p e k f", e=E, k=2)[:, :, k, :]
                dve.wait_ge(s_w1_hi, 1)
                low(by_expert(w1s, 1), wraw[:].rearrange("p (e f) -> p e f", e=E), scl[:, 0:1], by_expert(w1s, 0), s_w1_lo)
                dve.wait_ge(s_b1_hi, 1)
                low(b1s[32:40, :], b1raw[32:40, :], scl[32:40, 6:7], b1h[32:40, :], s_b1_lo)
                dve.wait_ge(s_b2_hi, 1)
                low(b2s[32:40, :], b2raw[32:40, :], scl[32:40, 12:13], b2h[32:40, :], s_b2_lo)
                dve.wait_ge(s_w2_hi, 1)
                low(by_expert(w2s, 1), wraw2[:].rearrange("p (e f) -> p e f", e=E), scl[:, 1:2], by_expert(w2s, 0), s_w2_lo)

            def statistics(tile, lo, m, eps, done):
                for j in range(m):
                    last = v.bn_stats(st[:, lo + j, :], tile(j))
                link(last)
                W = [lnw[:, k, lo:lo + m] for k in range(8)]
                me, qe, mo, qo = (st[:, lo:lo + m, k] for k in (1, 2, 4, 5))
                v.tensor_tensor(W[1], qe, qo, ALU.add)
                v.tensor_tensor(W[2], me, mo, ALU.add)
                link(v.tensor_tensor(W[0], me, mo, ALU.subtract))
                link(v.scalar_tensor_tensor(W[0], W[0], float(D // 4), W[0], ALU.mult, ALU.mult))
                link(v.tensor_tensor(W[0], W[0], W[1], ALU.add))
                link(v.tensor_scalar(W[0], W[0], 1.0 / D, eps, ALU.mult, ALU.add))
                ib = lni[:, lo:lo + m]
                link(v.tensor_scalar(ib, W[0].bitcast(I32), 1, None, ALU.logical_shift_right))
                link(v.tensor_scalar(W[5].bitcast(I32), ib, -1.0, float(0x5F3759DF), ALU.mult, ALU.add))
                for _ in range(3):
                    link(v.scalar_tensor_tensor(W[3], W[5], -0.5, W[5], ALU.mult, ALU.mult))
                    link(v.tensor_tensor(W[3], W[3], W[0], ALU.mult))
                    link(v.scalar_tensor_tensor(W[5], W[3], 1.5, W[5], ALU.add, ALU.mult))
                v.scalar_tensor_tensor(W[6], W[2], -0.5, W[5], ALU.mult, ALU.mult).then_inc(done, 1)

            def rowsplit(f, b):
                i = f * B + b
                dve.wait_ge(s_xhi, i + 1)
                dst = xs[:, b * J:(b + 1) * J, :]
                v.scalar_tensor_tensor(dst[:, :, D:2 * D], xn[:, b % 2], XS, dst[:, :, 0:D], ALU.mult,
                                       ALU.subtract).then_inc(s_xs_rows, 1)

            def route(f, bs):
                q, nb = r_index(f, bs), len(bs)
                lo, hi, m = bs[0] * J, (bs[-1] + 1) * J, nb * J
                b0_, b1_ = bs[0], bs[-1] + 1
                if f == 0:
                    for b in bs:
                        dve.wait_ge(x_in[b], 16)
                statistics(lambda j: x[:, lo + j, :], lo, m, EPS_FFN, s_route_stats)
                dve.wait_ge(s_route_stats, q + 1)
                for b0 in bs[::2]:
                    b, i = b0 + 1, f * B + b0 + 1
                    if i >= 2:
                        dve.wait_ge(s_xs_rows, i - 1)
                    for j in range(J):
                        c = b * J + j
                        last = v.tensor_scalar(xn[:, 1, j, :], x[:, c, :], lnw[:, 5, c:c + 1], lnw[:, 6, c:c + 1], ALU.mult, ALU.add)
                    last.then_inc(s_xn[1], 1)
                    dve.wait_ge(s_xnT_ps, i + 1)
                    if i >= 2:
                        dve.wait_ge(s_logits, i - 1)
                    for k in range(2):
                        last = v.tensor_copy(xnT[1][:, k * 512:(k + 1) * 512], AT[1].bank[k])
                    last.then_inc(s_xnT_sb[1], 1)
                    rowsplit(f, b0)
                    rowsplit(f, b)
                n0, n1 = f * B + b0_, f * B + b1_

                def grid(a):
                    return a.rearrange("p (b j) -> p b j", b=nb)

                def over(a):
                    return a.unsqueeze(2).broadcast_to([P, m, E])

                def mask(k):
                    return masks[:, b0_:b1_, :, k * J:(k + 1) * J].rearrange("p b e j -> p b j e")

                def by_batch(a):
                    return a.rearrange("p (b j) e -> p b j e", b=nb)
                Z, EZ, T = (zl[:, k, lo:hi, :] for k in range(3))
                m1, s1, m2, e2, c1, rs = (small[:, k, lo:hi] for k in range(6))
                dve.wait_ge(s_logits, f * B + bs[-1] + 1)
                lg = LB[2][:, lo * E:hi * E].rearrange("p (j e) -> p j e", e=E)
                link(v.tensor_reduce(m1, lg, AX, ALU.max))
                v.tensor_tensor(Z, lg, over(m1), ALU.subtract).then_inc(s_zs, 1)
                dve.wait_ge(s_zs, q + 1)

                def first_of(eqm, k):
                    link(v.tensor_tensor(eqm, eqm, rev[:].unsqueeze(1).broadcast_to([P, m, E]), ALU.mult))
                    link(v.tensor_reduce(c1, eqm, AX, ALU.max))
                    link(v.tensor_tensor(mask(k), by_batch(eqm), grid(c1).unsqueeze(3).broadcast_to([P, nb, J, E]), ALU.is_equal))

                link(v.tensor_scalar(T, Z, 0.0, None, ALU.is_ge))
                first_of(T, 0)
                for k in range(nb):
                    last = v.scalar_tensor_tensor(by_batch(T)[:, k], mask(0)[:, k], -3.0e38, by_batch(Z)[:, k], ALU.mult, ALU.add)
                link(last)
                v.tensor_reduce(m2, T, AX, ALU.max).then_inc(s_z2, 1)
                dve.wait_ge(s_z2, q + 1)
                link(v.tensor_tensor(T, T, over(m2), ALU.is_equal))
                first_of(T, 1)
                mf, inf, kf = (t[:].rearrange("p b e c -> p (b e c)") for t in (masks, incl, masks))
                w0, w1_ = b0_ * E * NC, b1_ * E * NC
                v.tensor_tensor_scan(inf[:, w0:w1_], keep[:, 0:w1_ - w0], mf[:, w0:w1_], 0.0, ALU.mult, ALU.add)\
                    .then_inc(s_tile_counts, 1)
                dve.wait_ge(s_ez, q + 1)
                link(v.tensor_reduce(s1, EZ, AX, ALU.add))
                link(v.reciprocal(rs, s1))
                v.tensor_scalar(g12[:, n0:n1, 0:J], grid(rs), 0.5, None, ALU.mult)
                dve.wait_ge(s_e2, q + 1)
                v.scalar_tensor_tensor(g12[:, n0:n1, J:NC], grid(rs), 0.5, grid(e2), ALU.mult, ALU.mult)
                dve.wait_ge(s_prefix, q + 1)
                C = [cnt[:, k, b0_:b1_, :] for k in range(6)]
                flat = [c.rearrange("p b e -> p (b e)") for c in C]
                base = LB[3][:, b0_ * E:b1_ * E].rearrange("p (b e) -> p b e", e=E)
                total = LB[3][:, (B + b0_) * E:(B + b1_) * E].rearrange("p (b e) -> p b e", e=E)
                v.tensor_copy(C[4], base)
                cm = cmp[:, b0_:b1_, :, :].rearrange("p b e k -> p (b e) k")
                link(v.tensor_tensor(cm, total.rearrange("p b e -> p (b e)").unsqueeze(2).broadcast_to([P, nb * E, J]),
                                     thr[:].unsqueeze(1).broadcast_to([P, nb * E, J]), ALU.is_gt))
                link(v.tensor_reduce(flat[0], cm, AX, ALU.add))
                link(v.tensor_tensor_scan(flat[1], keep8[:, 0:nb, :].rearrange("p b e -> p (b e)"), flat[0], 0.0, ALU.mult, ALU.add))
                v.scalar_tensor_tensor(C[2], C[0], -float(P), C[4], ALU.mult, ALU.add)
                link(v.tensor_tensor(cmpt[:, b0_:b1_], cnt[0:1, 1, b0_:b1_, :].unsqueeze(2).broadcast_to([1, nb, NTP, E]),
                                     tnum[0:1, :].unsqueeze(1).unsqueeze(3).broadcast_to([1, nb, NTP, E]), ALU.is_le))
                v.scalar_tensor_tensor(C[3], C[1], float(P), C[2], ALU.mult, ALU.add)
                link(v.tensor_reduce(eidf[:, b0_:b1_, :].rearrange("p b t -> p (b t)"),
                                     cmpt[:, b0_:b1_].rearrange("p b t e -> p (b t) e"), AX, ALU.add))
                pos, inc, msk = (t[:, b0_:b1_] for t in (mpos, incl, masks))
                ef, ew = eidf[:, b0_:b1_, :], eidw[:, b0_:b1_, :]
                v.tensor_scalar(ef, ef, float(E - 1), None, ALU.min)
                link(v.tensor_tensor(pos.rearrange("p b e c -> p (b e) c"), inc.rearrange("p b e c -> p (b e) c"),
                                     flat[3].unsqueeze(2).broadcast_to([P, nb * E, NC]), ALU.add))
                v.scalar_tensor_tensor(ew, ef[:, :, 2:NT + 2], float(E), ef[:, :, 1:NT + 1], ALU.mult, ALU.add)
                link(v.tensor_tensor(pos, pos, msk, ALU.mult))
                e0 = n0 * NT
                v.scalar_tensor_tensor(eids[:, e0:e0 + nb * NT].rearrange("p (b t) -> p b t", b=nb), ew, float(E),
                                       ef[:, :, 0:NT], ALU.mult, ALU.add).then_inc(s_eids, 1)
                pr, pf = posr[:, b0_:b1_, :], [posf[:, k, b0_:b1_, :] for k in range(3)]
                link(v.tensor_reduce(pr, pos.rearrange("p b e c -> p b c e"), AX, ALU.add))
                link(v.tensor_scalar(pf[0], pr, -1.0, float(SLOTS - 1), ALU.add, ALU.min))
                v.tensor_scalar(pf[1], pf[0], 7, None, ALU.logical_shift_right)
                link(v.tensor_scalar(pf[2], pf[0], P - 1, None, ALU.bitwise_and))
                v.scalar_tensor_tensor(rows[:, n0:n1, :], pf[2], float(NT), pf[1], ALU.mult, ALU.add).then_inc(s_pos, nb)

            def ffn(i):
                g0 = i * NT

                def columns(t, p):
                    dve.wait_ge(s_xT_ps, t + (g0 + 1))
                    v.tensor_copy(xT[:, p, :], xTp[:, 0:2 * P]).then_inc(s_xT_sb, 1)

                def low(t, p):
                    dve.wait_ge(s_h_hi, t + (g0 + 1))
                    v.scalar_tensor_tensor(hl[:, p, :], hp[p][:], 0.0, hh[:, p, :], ALU.max, ALU.subtract).then_inc(s_h_lo, 1)

                def first():
                    columns(0, 0)
                    columns(1, 1)
                    low(0, 0)

                def step(t, p):
                    if not beyond(t + 2):
                        columns(t + 2, p)
                    if not beyond(t + 1):
                        low(t + 1, 1 - p)

                def two_steps(t):
                    step(t, 1)
                    step(t + 1, 0)

                steps(dve, first, two_steps, step)

            def combine(i):
                b = i % B
                for k in range(TOPK):
                    dve.wait_ge(gathered[i % 2][k], 16 * J * (i // 2 + 1))
                    for j in range(J):
                        c = k * J + j
                        last = v.scalar_tensor_tensor(xb(b)[:, j, :], yg[i % 2][:, c, :], g12[:, i, c:c + 1], xb(b)[:, j, :],
                                                      ALU.mult, ALU.add)
                    if k == 0:
                        link(last)
                last.then_inc(s_comb, 1)
                dve.wait_ge(s_comb, i + 1)

            def attend(bs):
                for i in range(2):
                    dve.wait_ge(scattered[i], 16 * NC * (2 if bs[0] == 0 else 3))
                def inputs(b, t):
                    combine(b)
                    statistics(lambda j: xb(b)[:, j, :], b * J, J, EPS_FFN, s_attn_stats)

                def features(b, t):
                    for i, ready, bank, done in ((1, s_ek, 2, s_fk), (0, s_eq, 0, s_fq)):
                        dve.wait_ge(ready, b + 1)
                        for k in range(2):
                            last = v.scalar_tensor_tensor(t.qk[:, i, 4 * k:4 * k + 4, :], t.exps[:, 4 * k:4 * k + 4, :], 1.0,
                                                          t.tiles(bank + k), ALU.min, ALU.max)
                        last.then_inc(done, 1)

                def dots(b, t):
                    dve.wait_ge(s_fq, b + 1)
                    dve.wait_ge(s_fk, b + 1)
                    link(v.tensor_tensor(t.tmp[:, 1], t.qk[:, 0], t.qk[:, 1], ALU.mult))
                    link(v.tensor_reduce(t.qks, t.tmp[:, 1].rearrange("p j (h e) -> p j h e", e=DH), AX, ALU.add))
                    link(v.tensor_scalar(t.qks, t.qks, EPS_QK, None, ALU.add))
                    link(v.reciprocal(t.rq, t.qks))

                def states(b, t):
                    dve.wait_ge(s_s_ps, b + 1)
                    v.tensor_tensor(t.sbd, t.bank[2][:, 0:P], headmask[:], ALU.mult).then_inc(s_s_sb, 1)

                betab, gammab = (brow[:, k, :].unsqueeze(1).broadcast_to([P, J, D]) for k in (4, 3))

                def beta_added(b, t):
                    link(v.tensor_tensor(xb(b), xb(b), betab, ALU.add))

                def heads(b, t):
                    dve.wait_ge(s_o_ps, b + 1)
                    for k in range(2):
                        last = v.tensor_tensor(t.tmp[:, 1, 4 * k:4 * k + 4, :].rearrange("p j (h e) -> p (j h) e", e=DH),
                                               t.bank[k].rearrange("p (g e) -> p g e", e=DH),
                                               t.rq[:, 4 * k:4 * k + 4, :].rearrange("p j h -> p (j h)").unsqueeze(2)
                                               .broadcast_to([P, 4 * H, DH]), ALU.mult)
                    last.then_inc(s_o_sb, 1)

                def outputs(b, t):
                    dve.wait_ge(s_wo_ps, b + 1)
                    statistics(lambda j: t.tiles(2 + j // 4)[:, j % 4, :], b * J, J, EPS_ATTN_OUT, s_attn_stats)

                def residual(b, t):
                    dve.wait_ge(s_yn, b + 1)
                    link(v.tensor_tensor(t.tmp[:, 1], t.tmp[:, 1], gammab, ALU.mult))
                    v.tensor_tensor(xb(b), xb(b), t.tmp[:, 1], ALU.add).then_inc(s_x2, 1)
                    dve.wait_ge(s_x2, b + 1)

                first, second = [(b, AT[b % 2]) for b in bs]
                inputs(*first)
                inputs(*second)
                features(*first)
                dots(*first)
                beta_added(*first)
                beta_added(*second)
                features(*second)
                states(*first)
                dots(*second)
                states(*second)
                for step in (heads, outputs, residual):
                    step(*first)
                    step(*second)

            def finish(b):
                combine(B + b)

            def fold_biases():
                dve.wait_ge(s_brow_in, 16 * 5)
                dve.wait_ge(s_bf_ps, 1)
                v.tensor_tensor(bvcol[:], LB[3][:, 2 * D:2 * D + 1], bcol[:, 3:4], ALU.add)
                link(v.scalar_tensor_tensor(rowrest[:, 0:2, :], LB[3][:, 0:2 * D].rearrange("p (i d) -> p i d", i=2), 1.0,
                                            brow[:, 0:2, :], ALU.add, ALU.add))
                link(v.tensor_copy(rowrest[:, 2, :], brow[:, 2, :]))
                for r in (0, 32, 64):
                    link(v.tensor_copy(rowpart[:], rowrest[:]))
                    v.tensor_copy(rows3[r:r + 1], rowpart[r:r + 1])
                    link(v.tensor_tensor(rowrest[:], rowrest[:], rowpart[:], ALU.subtract))
                v.tensor_copy(rows3[64:65], rowpart[64:65]).then_inc(s_bf_sb, 1)

            setup()
            for job in PLAN:
                if job[0] == "R":
                    route(job[1], job[2])
                elif job[0] == "W":
                    split_weights()
                    fold_biases()
                elif job[0] == "C":
                    ffn(job[1])
                elif job[0] == "M":
                    attend(job[1])
                else:
                    finish(job[1])


def kernel(**inputs):
    import numpy as _np
    import concourse.bacc as _bacc
    from concourse import mybir as _mybir
    from concourse.bass_utils import run_bass_kernel_spmd as _run

    names = ["L0_attn_" + n for n in ("x", "Wq", "bq", "Wk", "bk", "Wv", "bv", "Wq2", "bq2", "Wk2", "bk2", "Wv2", "bv2",
                                      "Wo", "bo", "gamma", "beta")]
    names += ["L0_ffn_" + n for n in ("gate_w", "w1", "b1", "w2", "b2")]
    nc = _bacc.Bacc("TRN2", target_bir_lowering=False, num_devices=1)
    arrays, args = {}, []
    for name in names:
        a = _np.ascontiguousarray(inputs[name])
        arrays[f"in_{name}_dram"] = a
        args.append(nc.dram_tensor(f"in_{name}_dram", a.shape, _mybir.dt.from_np(a.dtype), kind="ExternalInput").ap())
    args.append(nc.dram_tensor("out_dram", (B, L, D), _mybir.dt.float32, kind="ExternalOutput").ap())
    macaron(nc, *args)
    r = _run(nc, [arrays], core_ids=[0])
    return r.results[0]["out_dram"]
```

```python
from contextlib import ExitStack

import concourse.bass as bass
from concourse import mybir

P = 128
B, L, D = 4, 1024, 128
E, F, TOPK = 8, 512, 2
H, DH = 16, 8
J = L // P
NC = TOPK * J
PB = 2
NQ = 2 * B // PB
NCP = PB * NC
PAIRS = PB * L * TOPK
FC = F // P
NT = (PAIRS - E) // P + E
SLOTS = NT * P
ET = PB * L // P
TURN = 4
NTP = NT + TURN
ROW = 2 * D + 8
PARTS = [(0, 8), (8, 20), (20, 32), (32, NT)]
CUTS = [lo - 3 for lo, _ in PARTS[1:]]
SEL = 256.0
XS = 16.0
EPS_FFN, EPS_ATTN_OUT, EPS_QK = 1e-5, 1e-3, 1e-6

ALU = mybir.AluOpType
ACT = mybir.ActivationFunctionType
AX = mybir.AxisListType.X
F32, F16, I32 = mybir.dt.float32, mybir.dt.float16, mybir.dt.int32
U32, U8, BF16 = mybir.dt.uint32, mybir.dt.uint8, mybir.dt.bfloat16
HALF = 2
RMAX = bass.bass_isa.ReduceOp.max



def macaron(nc, A_x, Wq, bq, Wk, bk, Wv, bv, Wq2, bq2, Wk2, bk2, Wv2, bv2, Wo, bo, gamma, beta,
            gate_w, w1, b1, w2, b2, out):
    with ExitStack() as ctx:
        def sb(name, shape, dt=F32):
            return ctx.enter_context(nc.sbuf_tensor(name, shape, dt))

        def ps(name, shape, dt=F32):
            return ctx.enter_context(nc.psum_tensor(name, shape, dt))

        def sem(name):
            return ctx.enter_context(nc.semaphore(name))

        s_w1_in = sem("w1_in")
        s_w2_in = sem("w2_in")
        s_w1_last_in = sem("w1_last_in")
        s_w1_less = sem("w1_less")
        s_b2_in = sem("b2_in")
        s_gate_in = sem("gate_in")
        s_wqkv_in = sem("wqkv_in")
        s_wqkv2_in = sem("wqkv2_in")
        s_wo_in = sem("wo_in")
        s_bcol_in = sem("bcol_in")
        s_brow_in = sem("brow_in")
        s_blank = sem("blank")
        s_consts = sem("consts")
        s_dve_order = sem("dve_order")
        s_absmax = sem("absmax")
        s_absmax_row = sem("absmax_row")
        s_largest = sem("largest")
        s_largest_all = sem("largest_all")
        s_scales = sem("scales")
        s_w1_hi = sem("w1_hi")
        s_w2_hi = sem("w2_hi")
        s_w1_lo = sem("w1_lo")
        s_w2_lo = sem("w2_lo")
        s_b2_hi = sem("b2_hi")
        s_b2_lo = sem("b2_lo")
        s_sel16 = sem("sel16")
        s_gate_ps = sem("gate_ps")
        s_gate_sb = sem("gate_sb")
        s_wT_ps = sem("wT_ps")
        s_wT_sb = sem("wT_sb")
        s_wf_ps = sem("wf_ps")
        s_wf_sb = sem("wf_sb")
        s_bf_ps = sem("bf_ps")
        s_bf_sb = sem("bf_sb")
        s_route_stats = sem("route_stats")
        s_attn_stats = sem("attn_stats")
        s_xn = sem("xn")
        s_xhi = sem("xhi")
        s_xs_rows = sem("xs_rows")
        s_xnT_ps = sem("xnT_ps")
        s_xnT_sb = sem("xnT_sb")
        s_logits = sem("logits")
        s_zs = sem("zs")
        s_ez = sem("ez")
        s_e2 = sem("e2")
        s_z2 = sem("z2")
        s_tile_counts = sem("tile_counts")
        s_prefix = sem("prefix")
        s_eids = sem("eids")
        s_pos = sem("pos")
        s_xT_ps = sem("xT_ps")
        s_xT_sb = sem("xT_sb")
        s_h_ps = sem("h_ps")
        s_h_hi = sem("h_hi")
        s_h_lo = sem("h_lo")
        s_y_ps = sem("y_ps")
        s_y_sb = sem("y_sb")
        s_added = sem("added")
        s_half_added = sem("half_added")
        s_ids = sem("ids")
        s_kept = sem("kept")
        s_comb = sem("comb")
        s_xa = [sem("xa_even"), sem("xa_odd")]
        s_xaT_ps = sem("xaT_ps")
        s_xaT_sb = sem("xaT_sb")
        s_v_ps = sem("v_ps")
        s_v_sb = sem("v_sb")
        s_q_ps = sem("q_ps")
        s_k_ps = sem("k_ps")
        s_eq = sem("eq")
        s_ek = sem("ek")
        s_fq = sem("fq")
        s_fk = sem("fk")
        s_s_ps = sem("s_ps")
        s_s_sb = sem("s_sb")
        s_o_ps = sem("o_ps")
        s_o_sb = sem("o_sb")
        s_oT_ps = sem("oT_ps")
        s_oT_sb = sem("oT_sb")
        s_res_ps = sem("res_ps")
        s_wo_ps = sem("wo_ps")
        s_yn = sem("yn")
        s_x2 = sem("x2")
        s_beta = sem("beta")
        s_out_stored = sem("out_stored")

        s_xn = [sem("xn_even"), sem("xn_odd")]
        s_xnT_sb = [sem("xnT_sb_even"), sem("xnT_sb_odd")]
        x_in = [sem(f"x_in{b}") for b in range(B)]
        blanked = [sem(f"blanked{q}") for q in range(NQ)]
        scattered = [[sem(f"scattered{q}{k}") for k in range(PB)] for q in range(NQ)]
        gathered = [sem(f"gathered{i}") for i in range(2)]
        rest_gathered = [sem(f"rest_gathered{i}") for i in range(2)]
        slots_in = [sem(f"slots_in{k}") for k in range(len(PARTS))]
        y_out = [sem(f"y_out{k}") for k in range(len(PARTS))]

        xs_dram = [nc.dram_tensor(f"xs_dram{q}", [SLOTS, ROW], F16).ap() for q in range(NQ)]
        y_dram = [nc.dram_tensor(f"y_dram{q}", [PAIRS + SLOTS, D], F32).ap() for q in range(NQ)]

        x = sb("x", [P, B * J, D])
        x_flat = x[:].rearrange("p j d -> p (j d)")
        w1_bytes = sb("w1_bytes", [P, E * 2 * F * HALF], U8)
        w2_bytes = sb("w2_bytes", [P, E * 2 * F * HALF], U8)
        w1s, w2s = w1_bytes[:].bitcast(F16), w2_bytes[:].bitcast(F16)
        wraw = sb("wraw", [P, E * F])
        wraw2 = sb("wraw2", [P, E * F])
        sel_bytes = sb("sel_bytes", [P, E * P * HALF], U8)
        sel = sel_bytes[:].bitcast(F16)
        b2raw = sb("b2raw", [40, D])
        b2s = sb("b2s", [P, D], F16)
        b2h = sb("b2h", [40, D], F16)
        pick16 = sb("pick16", [P, 40], F16)
        gate_sb = sb("gate_sb", [E, D])
        gateT = sb("gateT", [P, E])
        wq_sb = sb("wq_sb", [P, 3, D])
        wqT = sb("wqT", [P, 3, D])
        wq2_sb = sb("wq2_sb", [P, 3, D])
        wf = sb("wf", [P, 3, D])
        wo_sb = sb("wo_sb", [P, D])
        bcol = sb("bcol", [P, 4])
        brow = sb("brow", [P, 5, D])
        bvcol = sb("bvcol", [P, 1])
        rowpart = sb("rowpart", [P, 3, D], BF16)
        rowrest = sb("rowrest", [P, 3, D])
        rows3 = sb("rows3", [P, 3, D], BF16)
        ones3 = sb("ones3", [P, P], BF16)
        amax = sb("amax", [P, 3])
        scl = sb("scl", [P, 16])
        ident = sb("ident", [P, P])
        ident16 = sb("ident16", [P, P], F16)
        tri = sb("tri", [P, P])
        ones = sb("ones", [P, P])
        headmask = sb("headmask", [P, P])
        rev = sb("rev", [P, E])
        thr = sb("thr", [P, ET])
        tnum = sb("tnum", [P, NTP])
        keep = sb("keep", [P, E * NCP])
        minus1 = sb("minus1", [P, 1])
        amax_row = sb("amax_row", [3, 1])

        st = sb("st", [P, B * J, 6])
        lnw = sb("lnw", [P, 8, B * J])
        lni = sb("lni", [P, B * J], I32)
        xn = sb("xn", [P, 2, J, D])
        xnT_even = sb("xnT_even", [P, L])
        xs = sb("xs", [P, B * J, ROW], F16)
        zl = sb("zl", [P, 3, B * J, E])
        small = sb("small", [P, 8, B * J])
        masks = sb("masks", [P, E, NCP])
        incl = sb("incl", [P, E, NCP])
        mpos = sb("mpos", [P, E, NCP])
        cnt = sb("cnt", [P, 6, E])
        cmp = sb("cmp", [P, E, ET])
        cmpt = sb("cmpt", [1, NTP, E])
        eidf = sb("eidf", [1, NTP])
        eidw = sb("eidw", [1, NT])
        eids = sb("eids", [1, NQ * NT], I32)
        posf = sb("posf", [P, 3, NCP], I32)
        posr = sb("posr", [P, NCP])
        rows = sb("rows", [P, NQ, NCP], I32)
        g12 = sb("g12", [P, 2 * B, NC])

        xsort = sb("xsort", [P, NT, ROW], F16)
        xT = sb("xT", [P, 2, 2 * P], F16)
        hh = sb("hh", [P, 2, F], F16)
        hl = sb("hl", [P, 2, F], F16)
        yall = sb("yall", [P, NT, D])
        yg = [wraw2[:, 0:NC * D].rearrange("p (c d) -> p c d", c=NC), sb("yg1", [P, NC, D])[:]]
        sbd = sb("sbd", [P, 2, P])
        qks = sb("qks", [P, 2, J, H])
        rq = sb("rq", [P, 2, J, H])

        LB = [ps(f"LB{i}", [P, 512]) for i in range(4)]
        xTp = ps("xTp", [P, 1024], F16)
        hp = [ps(f"hp{i}", [P, 512]) for i in range(2)]
        yp = ps("yp", [P, 512])

        def grid(a):
            return a.rearrange("p (i j d) -> p i j d", i=2, j=J)

        class Attention:
            def __init__(self, wide, columns, banks, m):
                self.qk = wide[0]
                self.tmp = wide[1]
                self.xaT, self.vT = columns[:, 0:L], columns[:, L:2 * L]
                self.bank = banks
                self.exps = xn[:, m]
                self.sbd, self.qks, self.rq = sbd[:, m], qks[:, m], rq[:, m]

            def tiles(self, i):
                return self.bank[i].rearrange("p (j d) -> p j d", j=4)

        numbers = xs[:].bitcast(I32)[:, :, D:D + 1]
        slot_numbers = xsort[:].bitcast(I32)[:, :, D:D + 1]
        kept_numbers = sb("kept_numbers", [P, NQ, NT], I32)
        later_rows = xs[:].bitcast(F32)[:, 2 * J:, 0:D].rearrange("p (i j) d -> p i j d", i=2)
        AT = [Attention((grid(wraw2[:, NC * D:]), grid(wraw[:, 2 * L:])), wraw[:, 0:2 * L], [LB[i][:] for i in range(4)], 0),
              Attention((later_rows, grid(yg[1].rearrange("p c d -> p (c d)"))),
                        yall[:].rearrange("p t d -> p (t d)")[:, 0:2 * L], [hp[0][:], hp[1][:], yp[:], xTp[:].bitcast(F32)], 1)]

        def xnT(q):
            return [xnT_even[:], yg[1].rearrange("p c d -> p (c d)")[:, 0:L] if q < 2 else AT[1 - q % 2].vT]

        w1_last = yall[:].rearrange("p t d -> p (t d)")[:, 0:E * F]
        one_hi, one_lo = xs[:, :, D - 1:D], xs[:, :, 2 * D - 1:2 * D]

        def route_banks(q):
            even = AT[0].bank[0:2]
            return ([even, AT[1].bank[0:2]], LB[2], LB[1 if q == 1 else 3]) if q < NQ - 1 else ([even, AT[0].bank[2:4]], LB[0], LB[1])

        def loads(i):
            return [(0, J)] if i < 2 * B - PB else [(0, J // 2), (J // 2, J)]

        def pairs_place(i):
            return yall[:, NC:2 * NC, :] if i == 3 else yg[i % PB]

        def xb(b):
            return x[:, b * J:(b + 1) * J, :]

        PLAN = [("S", 0), ("N", 0), ("S", 1), ("X", 0), ("N", 1), ("K", 0), ("X", 1), ("W",), ("K", 1), ("L",), ("C", 0), ("C", 1),
                ("I", 0), ("M", 0), ("S", 2), ("N", 2), ("X", 2), ("T", 1), ("A", 1), ("K", 2), ("I", 1), ("M", 1),
                ("S", 3), ("N", 3), ("C", 2), ("C", 3), ("F",)]
        EARLY = 12
        ADD_AT = {1: 9, 3: 21}
        INPUT_AT = 33
        nth = [1, 2, 4, 3]
        SPLIT_BY_DVE = 1
        TURN_AT, COPY_AT, LOGITS_AT, CHOOSE_AT = 1, 3, 5, 9

        def batches(q):
            return [q % 2 * PB, q % 2 * PB + 1]

        def attentions(h):
            return sorted(batches(h), key=lambda b: nth[b])

        def steps(engine, first, turn, step, cuts, n=2):
            first()
            step(0, 0)
            starts = sorted({1, *cuts})
            for start, end in zip(starts, starts[1:] + [NT - 2]):
                for before in cuts.get(start, []):
                    before()
                if start < end:
                    with engine.Fori(start, end - n + 1, n) as t:
                        turn(t, n)
            turn(NT - 2, 2)

        def beyond(t):
            return isinstance(t, int) and t >= NT

        block = ctx.enter_context(nc.Block())

        @block.sync
        def _(sp):
            def load_x(b):
                sp.dma_start(xb(b), A_x[b].rearrange("(p j) h -> p j h", j=J)).then_inc(x_in[b], 16)

            load_x(0)
            load_x(1)
            sp.dma_start(gate_sb[:], gate_w).then_inc(s_gate_in, 16)
            w1_rows = wraw[:].rearrange("p (e f) -> p e f", e=E)
            sp.dma_start(w1_rows[0:D - 1], w1[:, 0:D - 1, :].rearrange("e p f -> p e f")).then_inc(s_w1_in, 16)
            sp.dma_start(w1_rows[D - 1:D], b1.rearrange("(a e) f -> a e f", a=1)).then_inc(s_w1_in, 16)
            load_x(2)
            load_x(3)
            sp.dma_start(w1_last.rearrange("p (e f) -> p e f", e=E),
                         w1[:, D - 1:D, :].rearrange("e a f -> a e f").broadcast_to([P, E, F])).then_inc(s_w1_last_in, 16)
            sp.wait_ge(s_blank, 2)

            def blank(q):
                sp.dma_start(xs_dram[q].rearrange("(p t) c -> p t c", t=NT), xsort[:]).then_inc(blanked[q], 16)

            blank(0)
            sp.dma_start(wraw2[:].rearrange("p (e c d) -> p e c d", e=E, c=FC),
                         w2.rearrange("e (c p) d -> p e c d", p=P)).then_inc(s_w2_in, 16)
            for r in (0, 32):
                sp.dma_start(b2raw[r:r + E, :], b2).then_inc(s_b2_in, 16)
            for i, w in enumerate((Wq, Wk, Wv)):
                sp.dma_start(wq_sb[:, i, :], w).then_inc(s_wqkv_in, 16)
            for i, w in enumerate((Wq2, Wk2, Wv2)):
                sp.dma_start(wq2_sb[:, i, :], w).then_inc(s_wqkv2_in, 16)
            for i, v in enumerate((bq, bk, bv, bv2)):
                sp.dma_start(bcol[:, i:i + 1], v.rearrange("(p a) -> p a", a=1)).then_inc(s_bcol_in, 16)
            for i, v in enumerate((bq2, bk2, bo, gamma, beta)):
                sp.dma_start(brow[:, i, :], v.rearrange("(a d) -> a d", a=1).broadcast_to([P, D])).then_inc(s_brow_in, 16)
            sp.dma_start(wo_sb[:], Wo).then_inc(s_wo_in, 16)

            for q in range(1, NQ - 1):
                blank(q)

            def load_slots(q):
                for landed in scattered[q]:
                    sp.wait_ge(landed, 16 * NC)
                if q == 0:
                    for k in range(NQ - 1):
                        sp.wait_ge(blanked[k], 16)
                src = xs_dram[q].rearrange("(p t) c -> p t c", t=NT)
                for k, (lo, hi) in enumerate(PARTS):
                    if q:
                        sp.wait_ge(s_xT_ps, NT * (q - 1) + hi)
                        sp.wait_ge(s_kept, q)
                    sp.dma_start(xsort[:, lo:hi, :], src[:, lo:hi, :]).then_inc(slots_in[k], 16)

            def load_y(i):
                q, k = i // PB, i % PB
                for (lo, hi), done in zip(PARTS, y_out):
                    sp.wait_ge(done, 16 * (hi - lo) * (q + 1))
                src = y_dram[q][k * L * TOPK:(k + 1) * L * TOPK, :].rearrange("(p c) d -> p c d", c=NC)
                for (lo, hi), done in zip(loads(i), (gathered, rest_gathered)):
                    pairs = slice(lo * TOPK, hi * TOPK)
                    sp.dma_start(pairs_place(i)[:, pairs, :], src[:, pairs, :]).then_inc(done[k], 16)

            def store_x(b, lo=0, hi=J):
                sp.dma_start(out[b].rearrange("(p j) h -> p j h", j=J)[:, lo:hi, :], xb(b)[:, lo:hi, :]).then_inc(s_out_stored, 16)

            load_slots(0)
            sp.dma_start(xs_dram[NQ - 1], xs_dram[NQ - 2]).then_inc(blanked[NQ - 1], 16)
            load_slots(1)
            load_y(0)
            load_y(1)
            sp.wait_ge(s_added, J)
            load_y(2)
            load_y(3)
            load_slots(2)
            sp.wait_ge(s_x2, 4)
            load_slots(3)
            load_y(4)
            load_y(5)
            sp.wait_ge(s_added, 2 * J)
            store_x(0)
            store_x(1)
            load_y(6)
            load_y(7)
            n = PB
            for b in batches(NQ - 1):
                for lo, hi in loads(B + b):
                    n += 1
                    sp.wait_ge(s_comb, n)
                    store_x(b, lo, hi)
            sp.wait_ge(s_out_stored, 16 * (n - PB + 2))

        @block.gpsimd
        def _(pool):
            g = nc.gpsimd
            n = 0

            def order(ins):
                nonlocal n
                n += 1
                ins.then_inc(s_consts, 1)
                pool.wait_ge(s_consts, n)

            g.memset(xsort[:].bitcast(I32), 0).then_inc(s_blank, 1)
            pool.wait_ge(s_blank, 1)
            g.iota(slot_numbers, [[1, NT]], base=PAIRS, channel_multiplier=NT).then_inc(s_blank, 1)
            g.memset(xs[:].bitcast(I32)[:, :, D + 1:], 0).then_inc(s_ids, 1)
            g.memset(one_hi, XS).then_inc(s_ids, 1)
            g.memset(one_lo, 0.0).then_inc(s_ids, 1)
            order(g.memset(ones[:], 1.0))
            order(g.affine_select(ident[:], ones[:], [[-1, P]], ALU.is_equal, 0.0, base=0, channel_multiplier=1))
            order(g.affine_select(tri[:], ones[:], [[1, P]], ALU.is_gt, 0.0, base=0, channel_multiplier=-1))
            hm = headmask[:].rearrange("p (h e) -> p h e", e=DH)
            order(g.affine_select(hm, ones[:].rearrange("p (h e) -> p h e", e=DH), [[-DH, H], [0, DH]], ALU.is_ge, 0.0,
                                  base=0, channel_multiplier=1))
            order(g.affine_select(hm, hm, [[DH, H], [0, DH]], ALU.is_ge, 0.0, base=DH - 1, channel_multiplier=-1))
            order(g.iota(rev[:], [[-1, E]], base=E, channel_multiplier=0, allow_small_or_imprecise_dtypes=True))
            order(g.iota(thr[:], [[P, ET]], base=0, channel_multiplier=0, allow_small_or_imprecise_dtypes=True))
            order(g.iota(tnum[:], [[1, NTP]], base=0, channel_multiplier=0, allow_small_or_imprecise_dtypes=True))
            order(g.memset(keep[:], 1.0))
            order(g.memset(keep[:].rearrange("p (g c) -> p g c", c=NCP)[:, :, 0:1], 0.0))
            order(g.tensor_copy(ident16[:], ident[:]))
            order(g.tensor_scalar(pick16[:], ident[:, 0:40], SEL, None, ALU.mult))
            g.tensor_tensor(sel.rearrange("p (e t) -> p e t", e=E), pick16[:, 0:E].unsqueeze(2).broadcast_to([P, E, P]),
                            pick16[:, 32:32 + E].unsqueeze(2).broadcast_to([P, E, P]), ALU.add).then_inc(s_sel16, 1)

            n_ids = 3

            def less_last():
                pool.wait_ge(s_w1_in, 32)
                pool.wait_ge(s_w1_last_in, 16)
                g.tensor_tensor(wraw[0:D - 1, :], wraw[0:D - 1, :], w1_last[0:D - 1, :], ALU.subtract).then_inc(s_w1_less, 1)

            def ones_again(q):
                nonlocal n_ids
                lo, hi = batches(q)[0] * J, (batches(q)[1] + 1) * J
                g.memset(one_hi[:, lo:hi], XS).then_inc(s_ids, 1)
                g.memset(one_lo[:, lo:hi], 0.0).then_inc(s_ids, 1)
                n_ids += 2

            def split_rows(q):
                for k, b in enumerate(batches(q)):
                    pool.wait_ge(s_xhi, PB * q + k + 1)
                    dst = xs[:, b * J:(b + 1) * J, :]
                    g.tensor_tensor(dst[:, :, D:2 * D - 1], xn[:, k, :, 0:D - 1], dst[:, :, 0:D - 1], ALU.subtract).then_inc(s_xs_rows, 1)

            def number(q, k, choice):
                nonlocal n_ids
                n_ids += 1
                b = batches(q)[k]
                g.iota(numbers[:, b * J:(b + 1) * J, :], [[TOPK, J]], base=k * L * TOPK + choice, channel_multiplier=NC)\
                    .then_inc(s_ids, 1)
                pool.wait_ge(s_ids, n_ids)

            def scatter_rows(q, k, choice):
                b = batches(q)[k]
                for j in range(J):
                    c = (k * TOPK + choice) * J + j
                    g.indirect_dma_start(
                        out=xs_dram[q], out_offset=bass.IndirectOffsetOnAxis(ap=rows[:, q, c:c + 1], axis=0),
                        in_=xs[:, b * J + j, :], in_offset=None).then_inc(scattered[q][k], 16)

            def scatter(q):
                if q == NQ - 2:
                    pool.wait_ge(blanked[q + 1], 16)
                """Rows of two batches to the slots of their tokens' first choices, then of their second."""
                pool.wait_ge(s_pos, q + 1)
                pool.wait_ge(s_xs_rows, PB * (q + 1))
                pool.wait_ge(blanked[q], 16)
                for k in range(PB):
                    if q >= 2:
                        pool.wait_ge(scattered[q - 2][k], 16 * NC)
                    number(q, k, 0)
                    scatter_rows(q, k, 0)
                for k in range(PB):
                    pool.wait_ge(scattered[q][k], 16 * J)
                    number(q, k, 1)
                    scatter_rows(q, k, 1)

            def keep_numbers(q):
                for landed in slots_in:
                    pool.wait_ge(landed, 16 * (q + 1))
                g.tensor_copy(kept_numbers[:, q, :].unsqueeze(2), slot_numbers).then_inc(s_kept, 1)
                pool.wait_ge(s_kept, q + 1)

            def scatter_results(q, start=0, end=NT):
                for (lo, hi), done in zip(PARTS, y_out):
                    for t in range(max(lo, start), min(hi, end)):
                        pool.wait_ge(s_y_sb, q * NT + t + 1)
                        g.indirect_dma_start(
                            out=y_dram[q], out_offset=bass.IndirectOffsetOnAxis(ap=kept_numbers[:, q, t:t + 1], axis=0),
                            in_=yall[:, t, :], in_offset=None).then_inc(done, 16)

            def beta_added(b):
                pool.wait_ge(s_brow_in, 16 * 5)
                pool.wait_ge(s_xa[b % 2], b // PB + 1)
                g.tensor_tensor(xb(b), xb(b), brow[:, 4, :].unsqueeze(1).broadcast_to([P, J, D]), ALU.add).then_inc(s_beta, 1)

            split_rows(0)
            less_last()
            scatter(0)
            scatter(1)
            keep_numbers(0)
            scatter_results(0)
            keep_numbers(1)
            scatter_results(1)
            for b in attentions(0):
                beta_added(b)
            split_rows(2)
            scatter(2)
            for b in attentions(1):
                beta_added(b)
            keep_numbers(2)
            split_rows(3)
            ones_again(3)
            scatter_results(2, 0, EARLY)
            scatter(3)
            scatter_results(2, EARLY)
            keep_numbers(3)
            scatter_results(3)

        @block.tensor
        def _(pe):
            mm, tr = nc.tensor.matmul, nc.tensor.transpose
            word = pe.alloc_register("experts_of_tiles")

            def setup():
                pe.wait_ge(s_consts, 10)
                pe.wait_ge(s_gate_in, 16)
                tr(LB[0][:, 0:E], gate_sb[:], ident[0:E, 0:E]).then_inc(s_gate_ps, 1)

            def fold():
                pe.wait_ge(s_wqkv_in, 16 * 3)
                for i in range(3):
                    last = tr(LB[1][:, i * D:(i + 1) * D], wq_sb[:, i, :], ident[:])
                last.then_inc(s_wT_ps, 1)
                pe.wait_ge(s_wT_sb, 1)
                pe.wait_ge(s_wqkv2_in, 16 * 3)
                for i in range(3):
                    last = mm(LB[1][:, i * D:(i + 1) * D], wqT[:, i, :], wq2_sb[:, i, :], start=True, stop=True)
                last.then_inc(s_wf_ps, 1)

            def fold_biases():
                pe.wait_ge(s_bcol_in, 16 * 4)
                for i in range(2):
                    mm(LB[3][:, i * D:(i + 1) * D], bcol[:, i:i + 1].broadcast_to([P, P]), wq2_sb[:, i, :], start=True, stop=True)
                mm(LB[3][:, 2 * D:2 * D + 1], wq2_sb[:, 2, :], bcol[:, 2:3], start=True, stop=True).then_inc(s_bf_ps, 1)

            def largest():
                pe.wait_ge(s_absmax, 1)
                pe.wait_ge(s_zs, 1)
                tr(LB[2][0:3, 0:P], amax[:], ident[:]).then_inc(s_absmax_row, 1)
                pe.wait_ge(s_largest, 1)
                mm(LB[2][:, 0:3], amax_row[:].broadcast_to([3, P]), ident[0:3, 0:3], start=True, stop=True).then_inc(s_largest_all, 1)

            def weights_ready():
                fold()
                largest()
                pe.wait_ge(s_eids, 1)
                fold_biases()

            def turn_rows(q):
                if q >= 2:
                    pe.wait_ge(s_x2, PB * (q - 1))
                else:
                    pe.wait_ge(s_gate_sb, 1)
                for p in (1, 0):
                    pe.wait_ge(s_xn[p], q + 1)
                    for j in range(J):
                        last = tr(route_banks(q)[0][p][j // 4][:, (j % 4) * P:(j % 4 + 1) * P], xn[:, p, j, :], ident[:])
                    last.then_inc(s_xnT_ps, 1)

            def logits(q):
                if q == 1:
                    pe.wait_ge(s_zs, 1)
                for p in (0, 1) if q == 0 else (1, 0):
                    b = batches(q)[p]
                    pe.wait_ge(s_xnT_sb[p], q + 1)
                    for j in range(J):
                        last = mm(route_banks(q)[1][:, (b * J + j) * E:(b * J + j + 1) * E], xnT(q)[p][:, j * P:(j + 1) * P], gateT[:],
                                  start=True, stop=True)
                    last.then_inc(s_logits, 1)

            def choose(q):
                if q == 1:
                    pe.wait_ge(s_wf_sb, 1)
                pe.wait_ge(s_tile_counts, q + 1)
                for k, lhs in enumerate((tri, ones)):
                    last = mm(route_banks(q)[2][:, k * E:(k + 1) * E], lhs[:], incl[:, :, NCP - 1], start=True, stop=True)
                last.then_inc(s_prefix, 1)

            def ffn(i):
                g0 = i * NT
                slots = xsort[:].rearrange("p t c -> p (t c)")

                def fetch(t):
                    pe.reg_load(word, eids[0:1, bass.ds(t + g0, 1)])

                def experts(n):
                    w = pe.snap(word)
                    return [pe.snap((w // E ** k if k else w) % E) for k in range(n)]

                def slot_rows(t):
                    return [slots[:, bass.ds(t * ROW + k * D, D)] for k in range(2)]

                def weights(table, e):
                    pick = sel_bytes[:, bass.ds(e * (P * HALF), P * HALF)].bitcast(F16)
                    return pick, [[table[:, bass.ds(e * (2 * F * HALF) + (part * F + c * P) * HALF, P * HALF)].bitcast(F16)
                                   for part in range(2)] for c in range(FC)]

                def address(aps, stationary):
                    for ap in aps:
                        pe.lower_ap(ap, for_matmul_weights=stationary)

                def turn(t, src):
                    for k in range(2):
                        last = tr(xTp[:, k * P:(k + 1) * P], src[k], ident16[:])
                    last.then_inc(s_xT_ps, 1)

                def up(t, p, w, src):
                    pe.wait_ge(s_xT_sb, t + (g0 + 1))
                    hi, lo = xT[:, p, 0:P], xT[:, p, P:2 * P]
                    for c, (wh, wl) in enumerate(w):
                        o = hp[p][:, c * P:(c + 1) * P]
                        mm(o, wh, hi, start=True, stop=False)
                        mm(o, wh, lo, start=False, stop=False)
                        last = mm(o, wl, hi, start=False, stop=True)
                        if c == 0 and not beyond(t + 1):
                            turn(t + 1, src)
                    last.then_inc(s_h_ps, 1)

                def down(t, p, pick, w):
                    if isinstance(t, int) and t == 0:
                        pe.wait_ge(s_h_hi, g0 + 1)
                    else:
                        pe.wait_ge(s_y_sb, t + g0)
                    for c, (wh, wl) in enumerate(w):
                        for part in (wh, wl):
                            mm(yp[:, 0:D], hh[:, p, c * P:(c + 1) * P], part, start=(c == 0 and part is wh), stop=False)
                    mm(yp[:, 0:D], pick, b2s[:], start=False, stop=False)
                    pe.wait_ge(s_h_lo, t + (g0 + 1))
                    for c, (wh, wl) in enumerate(w):
                        last = mm(yp[:, 0:D], hl[:, p, c * P:(c + 1) * P], wh, start=False, stop=(c == FC - 1))
                    last.then_inc(s_y_ps, 1)

                def one_step(t, p, e_now, e_next):
                    if not beyond(t + 1):
                        _, w1e = weights(w1_bytes, e_next)
                        address([part for chunk in w1e for part in chunk], True)
                    src = slot_rows(t + 2) if not beyond(t + 2) else []
                    address(src, True)
                    if not beyond(t + 1):
                        up(t + 1, 1 - p, w1e, src)
                    pick, w2e = weights(w2_bytes, e_now)
                    address([part for chunk in w2e for part in chunk], False)
                    address([pick], True)
                    down(t, p, pick, w2e)

                def step(t, p):
                    e = experts(2)
                    fetch(t + 1)
                    one_step(t, p, e[0], e[1])

                def turn_of(t, n):
                    e = experts(n + 1)
                    for k in range(n):
                        if k == 1 and not beyond(t + n):
                            fetch(t + n)
                        one_step(t + k, (1 + k) % 2, e[k], e[k + 1])

                def part_landed(k):
                    pe.wait_ge(slots_in[k], 16 * (i + 1))

                def first():
                    pe.wait_ge(s_eids, i + 1)
                    if i == 0:
                        pe.wait_ge(s_w1_hi, 1)
                        pe.wait_ge(s_w1_lo, 1)
                        pe.wait_ge(s_sel16, 1)
                    part_landed(0)
                    if i == 2:
                        pe.wait_ge(s_yn, B)
                    turn(0, slot_rows(0))
                    fetch(0)
                    up(0, 0, weights(w1_bytes, experts(1)[0])[1], slot_rows(1))
                    if i == 0:
                        pe.wait_ge(s_w2_hi, 1)
                        pe.wait_ge(s_b2_lo, 1)
                        pe.wait_ge(s_w2_lo, 1)

                cuts = {t: [lambda k=k: part_landed(k)] for k, t in enumerate(CUTS, 1)}
                if i == 2:
                    cuts.setdefault(TURN_AT, []).append(lambda: turn_rows(i + 1))
                    cuts.setdefault(LOGITS_AT, []).append(lambda: logits(i + 1))
                    cuts.setdefault(CHOOSE_AT, []).append(lambda: choose(i + 1))
                steps(pe, first, turn_of, step, cuts, TURN)

            def tile(t, j):
                return t.bank[j // 4][:, (j % 4) * P:(j % 4 + 1) * P]

            def attention_input(bs):
                for b in bs:
                    t = AT[b % 2]
                    pe.wait_ge(s_xa[b % 2], b // PB + 1)
                    for j in range(J):
                        last = tr(tile(t, j), t.tmp[:, 0, j, :], ident[:])
                    last.then_inc(s_xaT_ps, 1)

            def attend(bs):
                pe.wait_ge(s_wo_in, 16)

                def row(r):
                    return r.unsqueeze(1).broadcast_to([P, 4, D])

                def keys_and_queries(b, t):
                    pe.wait_ge(s_xaT_sb, nth[b])
                    if b == 2:
                        pe.wait_ge(s_pos, 3)
                    for i, bank, done in ((1, 2, s_k_ps), (0, 0, s_q_ps)):
                        for k in range(2):
                            mm(t.bank[bank + k], ones3[:], row(rows3[:, i, :]), start=True, stop=False)
                        for j in range(J):
                            last = mm(tile(t, 4 * bank + j), t.xaT[:, j * P:(j + 1) * P], wf[:, i, :], start=False, stop=(j % 4 == 3))
                        last.then_inc(done, 1)

                def states_and_values(b, t):
                    pe.wait_ge(s_fk, nth[b])
                    pe.wait_ge(s_fq, nth[b])
                    for j in range(J):
                        last = mm(t.bank[2][:, 0:P], t.qk[:, 1, j, :], t.qk[:, 0, j, :], start=(j == 0), stop=(j == J - 1))
                    last.then_inc(s_s_ps, 1)
                    for k in range(2):
                        last = mm(t.bank[k], wf[:, 2, :], t.xaT[:, k * 512:(k + 1) * 512], start=True, stop=True)
                    last.then_inc(s_v_ps, 1)

                def heads(b, t):
                    pe.wait_ge(s_s_sb, nth[b])
                    pe.wait_ge(s_v_sb, nth[b])
                    for j in range(J):
                        last = mm(tile(t, j), t.vT[:, j * P:(j + 1) * P], t.sbd, start=True, stop=True)
                    last.then_inc(s_o_ps, 1)

                def residual(b, t):
                    for k in range(2):
                        mm(t.bank[2 + k], ones3[:], row(rows3[:, 2, :]), start=True, stop=False)
                    for j in range(J):
                        last = mm(tile(t, J + j), t.xaT[:, j * P:(j + 1) * P], ident[:], start=False, stop=False)
                    last.then_inc(s_res_ps, 1)

                def head_columns(b, t):
                    pe.wait_ge(s_o_sb, nth[b])
                    for j in range(J):
                        last = tr(tile(t, j), t.tmp[:, 1, j, :], ident[:])
                    last.then_inc(s_oT_ps, 1)

                def output(b, t):
                    pe.wait_ge(s_oT_sb, nth[b])
                    for j in range(J):
                        last = mm(tile(t, J + j), t.xaT[:, j * P:(j + 1) * P], wo_sb[:], start=False, stop=(j % 4 == 3))
                    last.then_inc(s_wo_ps, 1)

                first, second = [(b, AT[b % 2]) for b in bs]
                for b in (first, second):
                    keys_and_queries(*b)
                for b in (first, second):
                    states_and_values(*b)
                heads(*first)
                heads(*second)
                for b in (first, second):
                    residual(*b)
                    head_columns(*b)
                output(*first)
                output(*second)

            setup()
            for job in PLAN:
                if job[0] == "N" and job[1] < NQ - 1:
                    turn_rows(job[1])
                elif job[0] == "X":
                    logits(job[1])
                elif job[0] == "I":
                    attention_input(attentions(job[1]))
                elif job[0] == "K":
                    choose(job[1])
                elif job[0] == "W":
                    weights_ready()
                elif job[0] == "C":
                    ffn(job[1])
                elif job[0] == "M":
                    attend(attentions(job[1]))

        @block.scalar
        def _(act):
            a = nc.scalar.activation

            def setup():
                act.wait_ge(s_gate_ps, 1)
                a(gateT[:], LB[0][:, 0:E], ACT.Copy, scale=1.0 / XS).then_inc(s_gate_sb, 1)

            def fold():
                act.wait_ge(s_wT_ps, 1)
                a(wqT[:].rearrange("p i d -> p (i d)"), LB[1][:, 0:3 * D], ACT.Copy).then_inc(s_wT_sb, 1)
                act.wait_ge(s_wf_ps, 1)
                a(wf[:].rearrange("p i d -> p (i d)"), LB[1][:, 0:3 * D], ACT.Copy).then_inc(s_wf_sb, 1)

            def split_weights():
                act.wait_ge(s_scales, 1)
                a(w1s.rearrange("p (e k f) -> p e k f", e=E, k=2)[:, :, 0, :], wraw[:].rearrange("p (e f) -> p e f", e=E),
                  ACT.Copy, scale=scl[:, 0:1]).then_inc(s_w1_hi, 1)
                a(b2s[0:E, :], b2raw[0:E, :], ACT.Copy, scale=scl[0:E, 12:13])
                a(b2h[32:40, :], b2raw[32:40, :], ACT.Copy, scale=scl[32:40, 12:13]).then_inc(s_b2_hi, 1)
                a(w2s.rearrange("p (e k f) -> p e k f", e=E, k=2)[:, :, 0, :], wraw2[:].rearrange("p (e f) -> p e f", e=E),
                  ACT.Copy, scale=scl[:, 1:2]).then_inc(s_w2_hi, 1)

            def normalise(dst, src, lo, last_sem, m=J):
                for j in range(m):
                    last = a(dst[:, j, :], src[:, j, :], ACT.Identity, scale=lnw[:, 5, lo + j:lo + j + 1],
                             bias=lnw[:, 6, lo + j:lo + j + 1])
                if last_sem is not None:
                    last.then_inc(last_sem, 1)

            def evacuate(dst, banks, sem):
                for k in range(2):
                    last = a(dst[:, k * 512:(k + 1) * 512], banks[k][:, :], ACT.Copy)
                last.then_inc(sem, 1)

            def normal_rows(q):
                b, odd = batches(q)
                act.wait_ge(s_route_stats, q + 1)
                if q:
                    act.wait_ge(s_xnT_ps, PB * q)
                    act.wait_ge(s_xs_rows, PB * q - 1)
                normalise(xn[:, 0], xb(b), b * J, s_xn[0])
                high_rows(q, b)

            def turned_rows(q):
                b, odd = batches(q)
                act.wait_ge(s_xnT_ps, PB * (q + 1))
                if q:
                    act.wait_ge(s_logits, PB * q - 1)
                evacuate(xnT(q)[0], AT[0].bank, s_xnT_sb[0])
                high_rows(q, odd)

            def choose(q):
                b, odd = batches(q)
                act.wait_ge(s_zs, q + 1)
                lo, hi = b * J, (odd + 1) * J
                a(zl[:, 1, lo:hi, :], zl[:, 0, lo:hi, :], ACT.Exp).then_inc(s_ez, 1)
                act.wait_ge(s_z2, q + 1)
                a(small[:, 3, lo:hi], small[:, 2, lo:hi], ACT.Exp).then_inc(s_e2, 1)

            def high_rows(q, b):
                act.wait_ge(s_xn[b % 2], q + 1)
                if q >= 2:
                    act.wait_ge(scattered[q - 2][b % 2], 16 * NC)
                a(xs[:, b * J:(b + 1) * J, 0:D - 1], xn[:, b % 2, :, 0:D - 1], ACT.Copy).then_inc(s_xhi, 1)

            def ffn(i):
                g0 = i * NT
                results = yall[:].rearrange("p t c -> p (t c)")

                def high(t, p):
                    act.wait_ge(s_h_ps, t + (g0 + 1))
                    a(hh[:, p, :], hp[p][:], ACT.Relu).then_inc(s_h_hi, 1)

                def part_free(k):
                    if i:
                        act.wait_ge(y_out[k], 16 * (PARTS[k][1] - PARTS[k][0]) * i)

                def result(t):
                    act.wait_ge(s_y_ps, t + (g0 + 1))
                    if isinstance(t, int) and t == 0:
                        part_free(0)
                    a(results[:, bass.ds(t * D, D)], yp[:, 0:D], ACT.Copy, scale=scl[:, 3:4]).then_inc(s_y_sb, 1)

                def step(t, p):
                    if not beyond(t + 1):
                        high(t + 1, 1 - p)
                    result(t)

                def two_steps(t):
                    step(t, 1)
                    step(t + 1, 0)

                cuts = {t: [lambda k=k: part_free(k)] for k, t in enumerate(CUTS, 1)}
                if i == 2:
                    cuts.setdefault(COPY_AT, []).append(lambda: turned_rows(i + 1))
                    cuts.setdefault(CHOOSE_AT, []).append(lambda: choose(i + 1))
                if i == 1:
                    b = attentions(0)[0]
                    for k in range(2):
                        cuts.setdefault(INPUT_AT + 2 * k, []).append(lambda k=k: attention_rows(b, k))
                steps(act, lambda: high(0, 0), lambda t, n: two_steps(t), step, cuts)

            def attention_rows(b, k):
                act.wait_ge(s_attn_stats, b // PB * 2 + 1)
                half = slice(4 * k, 4 * k + 4)
                normalise(AT[b % 2].tmp[:, 0, half], xb(b)[:, half, :], b * J + 4 * k, s_xa[b % 2] if k else None, 4)

            def attention_input(bs):
                def columns(b, t):
                    act.wait_ge(s_xaT_ps, nth[b])
                    if b % 2:
                        for (lo, hi), done in zip(PARTS, y_out):
                            act.wait_ge(done, 16 * (hi - lo) * PB)
                    evacuate(t.xaT, t.bank, s_xaT_sb)

                first, second = [(b, AT[b % 2]) for b in bs]
                columns(*first)
                columns(*second)

            def attend(bs):
                if bs[0]:
                    act.wait_ge(s_xs_rows, PB * 3)

                def exponentials(b, t, ready, bank, done):
                    act.wait_ge(ready, nth[b])
                    for k in range(2):
                        last = a(t.exps.rearrange("p j d -> p (j d)")[:, k * 512:(k + 1) * 512], t.bank[bank + k], ACT.Exp, bias=minus1[:])
                    last.then_inc(done, 1)

                def of_keys(b, t):
                    exponentials(b, t, s_k_ps, 2, s_ek)

                def of_queries(b, t):
                    act.wait_ge(s_fk, nth[b])
                    exponentials(b, t, s_q_ps, 0, s_eq)

                def values(b, t):
                    act.wait_ge(s_v_ps, nth[b])
                    for k in range(2):
                        last = a(t.vT[:, k * 512:(k + 1) * 512], t.bank[k], ACT.Identity, bias=bvcol[:])
                    last.then_inc(s_v_sb, 1)

                def head_columns(b, t):
                    act.wait_ge(s_oT_ps, nth[b])
                    act.wait_ge(s_res_ps, nth[b])
                    evacuate(t.xaT, t.bank, s_oT_sb)

                def outputs(b, t):
                    act.wait_ge(s_attn_stats, b // PB * 2 + 2)
                    for k in range(2):
                        normalise(t.tmp[:, 1, 4 * k:4 * k + 4, :], t.tiles(2 + k), b * J + 4 * k, s_yn if k else None, 4)

                first, second = [(b, AT[b % 2]) for b in bs]
                for step in (of_keys, of_queries):
                    step(*first)
                    step(*second)
                for step in (values, head_columns, outputs):
                    step(*first)
                    step(*second)

            setup()
            for job in PLAN:
                if job[0] == "N":
                    normal_rows(job[1])
                elif job[0] == "X":
                    turned_rows(job[1])
                elif job[0] == "A":
                    for b in attentions(job[1]):
                        for k in range(2):
                            attention_rows(b, k)
                elif job[0] == "I":
                    attention_input(attentions(job[1]))
                elif job[0] == "K":
                    choose(job[1])
                elif job[0] == "W":
                    fold()
                    split_weights()
                elif job[0] == "C":
                    ffn(job[1])
                elif job[0] == "M":
                    act.wait_ge(s_bf_sb, 1)
                    attend(attentions(job[1]))

        @block.vector
        def _(dve):
            v = nc.vector
            n = 0

            def link(ins):
                nonlocal n
                n += 1
                ins.then_inc(s_dve_order, 1)
                dve.wait_ge(s_dve_order, n)

            def setup():
                v.memset(minus1[:], -1.0)
                v.memset(b2s[:].bitcast(U32), 0)
                v.memset(rows3[:].bitcast(U32), 0)
                v.memset(ones3[:], 1.0)

            def power(src, dst, by):
                link(v.tensor_scalar(scl[:, src:src + 1], scl[:, src:src + 1], 1e-15, 1e15, ALU.max, ALU.min))
                bits = scl[:].bitcast(U32)
                link(v.tensor_scalar(bits[:, src:src + 1], bits[:, src:src + 1], 0x7F800000, 0x7F800000,
                                     ALU.bitwise_and, ALU.bitwise_xor))
                link(v.tensor_scalar(scl[:, dst:dst + 1], scl[:, src:src + 1], by, None, ALU.mult))

            def split_weights():
                link(v.memset(amax[:], 0.0))
                for k, (raw, landed, count, lanes) in enumerate(((wraw, s_w1_less, 1, P), (wraw2, s_w2_in, 16, P), (b2raw, s_b2_in, 32, E))):
                    dve.wait_ge(landed, count)
                    last = v.tensor_reduce(amax[0:lanes, k:k + 1], raw[0:lanes, :], AX, ALU.max, apply_absolute_value=True)
                last.then_inc(s_absmax, 1)
                dve.wait_ge(s_absmax_row, 1)
                v.tensor_reduce(amax_row[:], LB[2][0:3, 0:P], AX, ALU.max).then_inc(s_largest, 1)
                dve.wait_ge(s_largest_all, 1)
                link(v.tensor_copy(scl[:, 9:12], LB[2][:, 0:3]))
                link(v.tensor_scalar(scl[:, 4:5], scl[:, 9:10], float(D), None, ALU.mult))
                power(4, 0, 2.0 ** 8)
                link(v.tensor_scalar(scl[:, 2:3], scl[:, 0:1], XS, None, ALU.mult))
                link(v.scalar_tensor_tensor(scl[:, 5:6], scl[:, 2:3], 2.0 ** -10, scl[:, 11:12], ALU.mult, ALU.mult))
                link(v.tensor_tensor(scl[:, 5:6], scl[:, 5:6], scl[:, 10:11], ALU.max))
                power(5, 1, 2.0 ** 12)
                link(v.tensor_tensor(scl[:, 7:8], scl[:, 1:2], scl[:, 2:3], ALU.mult))
                v.reciprocal(scl[:, 3:4], scl[:, 7:8])
                v.tensor_scalar(scl[:, 12:13], scl[:, 7:8], 1.0 / SEL, None, ALU.mult).then_inc(s_scales, 1)

            def low_parts():
                def low(dst, raw, scale, high, done):
                    v.scalar_tensor_tensor(dst, raw, scale, high, ALU.mult, ALU.subtract).then_inc(done, 1)

                def by_expert(t, k):
                    return t.rearrange("p (e k f) -> p e k f", e=E, k=2)[:, :, k, :]
                dve.wait_ge(s_w1_hi, 1)
                low(by_expert(w1s, 1), wraw[:].rearrange("p (e f) -> p e f", e=E), scl[:, 0:1], by_expert(w1s, 0), s_w1_lo)
                dve.wait_ge(s_b2_hi, 1)
                low(b2s[32:40, :], b2raw[32:40, :], scl[32:40, 12:13], b2h[32:40, :], s_b2_lo)
                dve.wait_ge(s_w2_hi, 1)
                low(by_expert(w2s, 1), wraw2[:].rearrange("p (e f) -> p e f", e=E), scl[:, 1:2], by_expert(w2s, 0), s_w2_lo)

            def statistics(rows, lo, m, eps, done, tile=lambda: None, times=1.0):
                for j in range(m):
                    last = v.bn_stats(st[:, lo + j, :], rows(j))
                    if j % 8 == 7:
                        tile()
                link(last)
                W = [lnw[:, k, lo:lo + m] for k in range(8)]
                me, qe, mo, qo = (st[:, lo:lo + m, k] for k in (1, 2, 4, 5))
                v.tensor_tensor(W[1], qe, qo, ALU.add)
                v.tensor_tensor(W[2], me, mo, ALU.add)
                link(v.tensor_tensor(W[0], me, mo, ALU.subtract))
                link(v.scalar_tensor_tensor(W[0], W[0], float(D // 4), W[0], ALU.mult, ALU.mult))
                link(v.tensor_tensor(W[0], W[0], W[1], ALU.add))
                link(v.tensor_scalar(W[0], W[0], 1.0 / (D * times ** 2), eps / times ** 2, ALU.mult, ALU.add))
                tile()
                ib = lni[:, lo:lo + m]
                link(v.tensor_scalar(ib, W[0].bitcast(I32), 1, None, ALU.logical_shift_right))
                link(v.tensor_scalar(W[5].bitcast(I32), ib, -1.0, float(0x5F3759DF), ALU.mult, ALU.add))
                for _ in range(3):
                    link(v.scalar_tensor_tensor(W[3], W[5], -0.5, W[5], ALU.mult, ALU.mult))
                    link(v.tensor_tensor(W[3], W[3], W[0], ALU.mult))
                    link(v.scalar_tensor_tensor(W[5], W[3], 1.5, W[5], ALU.add, ALU.mult))
                    tile()
                v.scalar_tensor_tensor(W[6], W[2], -0.5, W[5], ALU.mult, ALU.mult).then_inc(done, 1)

            def rowsplit(i, b):
                dve.wait_ge(s_xhi, i + 1)
                dst = xs[:, b * J:(b + 1) * J, :]
                v.tensor_tensor(dst[:, :, D:2 * D - 1], xn[:, b % 2, :, 0:D - 1], dst[:, :, 0:D - 1], ALU.subtract).then_inc(s_xs_rows, 1)

            def row_statistics(q):
                b, odd = batches(q)
                lo = b * J
                if q < 2:
                    for k in (b, odd):
                        dve.wait_ge(x_in[k], 16)
                statistics(lambda j: x[:, lo + j, :], lo, PB * J, EPS_FFN, s_route_stats, times=XS)

            def normal_rows(q):
                b, odd = batches(q)
                i = PB * q + 1
                dve.wait_ge(s_route_stats, q + 1)
                if q:
                    dve.wait_ge(s_xs_rows, i - 1)
                for j in range(J):
                    c = odd * J + j
                    last = v.tensor_scalar(xn[:, 1, j, :], x[:, c, :], lnw[:, 5, c:c + 1], lnw[:, 6, c:c + 1], ALU.mult, ALU.add)
                last.then_inc(s_xn[1], 1)

            def turned_rows(q):
                b, odd = batches(q)
                i = PB * q + 1
                dve.wait_ge(s_xnT_ps, PB * q + 1)
                if q:
                    dve.wait_ge(s_logits, i - 1)
                for k in range(2):
                    last = v.tensor_copy(xnT(q)[1][:, k * 512:(k + 1) * 512], route_banks(q)[0][1][k])
                last.then_inc(s_xnT_sb[1], 1)
                if q == SPLIT_BY_DVE:
                    rowsplit(i - 1, b)
                    rowsplit(i, odd)

            def choose(q, tile=lambda: None):
                b, odd = batches(q)
                lo, hi, m = b * J, (odd + 1) * J, PB * J
                if q == 0:
                    dve.wait_ge(s_consts, 10)

                def grid(a):
                    return a.rearrange("p (b j) -> p b j", b=PB)

                def over(a):
                    return a.unsqueeze(2).broadcast_to([P, m, E])

                def mask(k):
                    return masks[:].rearrange("p e (b k j) -> p k b j e", b=PB, k=TOPK)[:, k]

                def by_batch(a):
                    return a.rearrange("p (b j) e -> p b j e", b=PB)
                Z, EZ, T = (zl[:, k, lo:hi, :] for k in range(3))
                m1, s1, m2, e2, c1, rs = (small[:, k, lo:hi] for k in range(6))
                dve.wait_ge(s_logits, PB * (q + 1))
                lg = route_banks(q)[1][:, lo * E:hi * E].rearrange("p (j e) -> p j e", e=E)
                link(v.tensor_reduce(m1, lg, AX, ALU.max))
                v.tensor_tensor(Z, lg, over(m1), ALU.subtract).then_inc(s_zs, 1)
                dve.wait_ge(s_zs, q + 1)

                def first_of(eqm, k):
                    link(v.tensor_tensor(eqm, eqm, rev[:].unsqueeze(1).broadcast_to([P, m, E]), ALU.mult))
                    link(v.tensor_reduce(c1, eqm, AX, ALU.max))
                    link(v.tensor_tensor(mask(k), by_batch(eqm), grid(c1).unsqueeze(3).broadcast_to([P, PB, J, E]), ALU.is_equal))

                link(v.tensor_scalar(T, Z, 0.0, None, ALU.is_ge))
                first_of(T, 0)
                tile()
                for k in range(PB):
                    last = v.scalar_tensor_tensor(by_batch(T)[:, k], mask(0)[:, k], -3.0e38, by_batch(Z)[:, k], ALU.mult, ALU.add)
                link(last)
                v.tensor_reduce(m2, T, AX, ALU.max).then_inc(s_z2, 1)
                dve.wait_ge(s_z2, q + 1)
                tile()
                link(v.tensor_tensor(T, T, over(m2), ALU.is_equal))
                first_of(T, 1)
                mf, inf = (t[:].rearrange("p e c -> p (e c)") for t in (masks, incl))
                v.tensor_tensor_scan(inf, keep[:], mf, 0.0, ALU.mult, ALU.add).then_inc(s_tile_counts, 1)
                for _ in range(2):
                    tile()
                dve.wait_ge(s_prefix, q + 1)
                C = [cnt[:, k, :] for k in range(5)]
                counts = route_banks(q)[2]
                v.tensor_copy(C[4], counts[:, 0:E])
                link(v.tensor_tensor(cmp[:], counts[:, E:2 * E].unsqueeze(2).broadcast_to([P, E, ET]),
                                     thr[:].unsqueeze(1).broadcast_to([P, E, ET]), ALU.is_gt))
                tile()
                link(v.tensor_reduce(C[0], cmp[:], AX, ALU.add))
                link(v.tensor_tensor_scan(C[1], ones[:, 0:E], C[0], 0.0, ALU.mult, ALU.add))
                v.scalar_tensor_tensor(C[2], C[0], -float(P), C[4], ALU.mult, ALU.add)
                link(v.tensor_tensor(cmpt[:], cnt[0:1, 1, :].unsqueeze(1).broadcast_to([1, NTP, E]),
                                     tnum[0:1, :].unsqueeze(2).broadcast_to([1, NTP, E]), ALU.is_le))
                v.scalar_tensor_tensor(C[3], C[1], float(P), C[2], ALU.mult, ALU.add)
                link(v.tensor_reduce(eidf[:], cmpt[:], AX, ALU.add))
                tile()
                v.tensor_scalar(eidf[:], eidf[:], float(E - 1), None, ALU.min)
                link(v.tensor_tensor(mpos[:], incl[:], C[3].unsqueeze(2).broadcast_to([P, E, NCP]), ALU.add))

                def horner(dst, src, k):
                    return v.scalar_tensor_tensor(dst, src, float(E), eidf[:, k:NT + k], ALU.mult, ALU.add)

                horner(eidw[:], eidf[:, TURN:NT + TURN], TURN - 1)
                link(v.tensor_tensor(mpos[:], mpos[:], masks[:], ALU.mult))
                horner(eidw[:], eidw[:], 2)
                tile()
                pf = [posf[:, k, :] for k in range(3)]
                link(v.tensor_reduce(posr[:], mpos[:].rearrange("p e c -> p c e"), AX, ALU.add))
                horner(eidw[:], eidw[:], 1)
                link(v.tensor_scalar(pf[0], posr[:], -1.0, float(SLOTS - 1), ALU.add, ALU.min))
                horner(eids[:, q * NT:(q + 1) * NT], eidw[:], 0).then_inc(s_eids, 1)
                v.tensor_scalar(pf[1], pf[0], 7, None, ALU.logical_shift_right)
                link(v.tensor_scalar(pf[2], pf[0], P - 1, None, ALU.bitwise_and))
                v.scalar_tensor_tensor(rows[:, q, :], pf[2], float(NT), pf[1], ALU.mult, ALU.add).then_inc(s_pos, 1)
                dve.wait_ge(s_ez, q + 1)
                link(v.tensor_reduce(s1, EZ, AX, ALU.add))
                link(v.reciprocal(rs, s1))
                gates = g12[:, PB * q:PB * (q + 1), :]
                v.tensor_scalar(gates[:, :, 0:J], grid(rs), 0.5, None, ALU.mult)
                dve.wait_ge(s_e2, q + 1)
                v.scalar_tensor_tensor(gates[:, :, J:NC], grid(rs), 0.5, grid(e2), ALU.mult, ALU.mult)

            def ffn(i):
                g0 = i * NT

                def columns(t, p):
                    dve.wait_ge(s_xT_ps, t + (g0 + 1))
                    v.tensor_copy(xT[:, p, :], xTp[:, 0:2 * P]).then_inc(s_xT_sb, 1)

                def low(t, p):
                    dve.wait_ge(s_h_hi, t + (g0 + 1))
                    v.scalar_tensor_tensor(hl[:, p, :], hp[p][:], 0.0, hh[:, p, :], ALU.max, ALU.subtract).then_inc(s_h_lo, 1)

                def first():
                    columns(0, 0)
                    columns(1, 1)
                    low(0, 0)

                def step(t, p):
                    if not beyond(t + 2):
                        columns(t + 2, p)
                    if not beyond(t + 1):
                        low(t + 1, 1 - p)

                def two_steps(t):
                    step(t, 1)
                    step(t + 1, 0)

                def add(j, k):
                    for b in range(PB):
                        xt = x_flat[:, bass.ds(j * D + b * J * D, D)]
                        yt = yg[b].rearrange("p c d -> p (c d)")[:, bass.ds(j * (TOPK * D) + k * D, D)]
                        last = v.scalar_tensor_tensor(xt, yt, g12[:, i // 2 * B + b, bass.ds(j + k * J, 1)], xt, ALU.mult, ALU.add)
                    return last

                def range_of(start, end):
                    with dve.Fori(start, end - 1, 2) as t:
                        two_steps(t)

                first()
                step(0, 0)
                t = 1

                def tile():
                    nonlocal t
                    step(t, t % 2)
                    t += 1

                if i == 0:
                    fold_biases(tile)
                    range_of(t, NT - 2)
                elif i == 2:
                    for _ in range(2):
                        tile()
                    turned_rows(i + 1)
                    for _ in range(2):
                        tile()
                    choose(i + 1, tile)
                    if t % 2 == 0:
                        tile()
                    range_of(t, NT - 2)
                else:
                    range_of(1, ADD_AT[i])
                    for b in range(PB):
                        dve.wait_ge(gathered[b], 16 * (i // 2 * PB + 1))
                    with dve.Fori(0, J) as j:
                        add(j, 0).then_inc(s_half_added, 1)
                        step(j * 2 + ADD_AT[i], 1)
                        dve.wait_ge(s_half_added, j + (i // 2 * J + 1))
                        add(j, 1).then_inc(s_added, 1)
                        step(j * 2 + (ADD_AT[i] + 1), 0)
                    t = ADD_AT[i] + PB * J
                    if i == 1:
                        dve.wait_ge(s_added, J)
                        statistics(lambda j: x[:, j, :], 0, PB * J, EPS_FFN, s_attn_stats, tile)
                        b = attentions(0)[1]
                        dve.wait_ge(s_attn_stats, 1)
                        for j in range(J):
                            c = b * J + j
                            last = v.tensor_scalar(AT[1].tmp[:, 0, j, :], x[:, c, :], lnw[:, 5, c:c + 1], lnw[:, 6, c:c + 1],
                                                   ALU.mult, ALU.add)
                            if j % 4 == 3:
                                tile()
                        last.then_inc(s_xa[1], 1)
                        if t % 2 == 0:
                            tile()
                    if t < NT - 2:
                        range_of(t, NT - 2)
                two_steps(NT - 2)

            n_sums = 0

            def combine(i):
                nonlocal n_sums
                b = i % B
                for (lo, hi), (landed, count) in zip(loads(i), ((gathered, i // PB + 1), (rest_gathered, 1))):
                    dve.wait_ge(landed[i % 2], 16 * count)
                    for k in range(TOPK):
                        for j in range(lo, hi):
                            c = k * J + j
                            last = v.scalar_tensor_tensor(xb(b)[:, j, :], pairs_place(i)[:, j * TOPK + k, :], g12[:, i, c:c + 1],
                                                          xb(b)[:, j, :], ALU.mult, ALU.add)
                        if k == 0:
                            link(last)
                    last.then_inc(s_comb, 1)
                    n_sums += 1
                dve.wait_ge(s_comb, n_sums)

            def input_statistics(h):
                statistics(lambda j: x[:, PB * J * h + j, :], PB * J * h, PB * J, EPS_FFN, s_attn_stats)

            def attend(bs):
                for landed in scattered[1]:
                    dve.wait_ge(landed, 16 * NC)

                def features(b, t, i, ready, bank, done):
                    dve.wait_ge(ready, nth[b])
                    for k in range(2):
                        last = v.scalar_tensor_tensor(t.qk[:, i, 4 * k:4 * k + 4, :], t.exps[:, 4 * k:4 * k + 4, :], 1.0,
                                                      t.tiles(bank + k), ALU.min, ALU.max)
                    last.then_inc(done, 1)

                def dots(b, t):
                    dve.wait_ge(s_fq, nth[b])
                    dve.wait_ge(s_fk, nth[b])
                    link(v.tensor_tensor(t.tmp[:, 1], t.qk[:, 0], t.qk[:, 1], ALU.mult))
                    link(v.tensor_reduce(t.qks, t.tmp[:, 1].rearrange("p j (h e) -> p j h e", e=DH), AX, ALU.add))
                    link(v.tensor_scalar(t.qks, t.qks, EPS_QK, None, ALU.add))
                    link(v.reciprocal(t.rq, t.qks))

                def states(b, t):
                    dve.wait_ge(s_s_ps, nth[b])
                    v.tensor_tensor(t.sbd, t.bank[2][:, 0:P], headmask[:], ALU.mult).then_inc(s_s_sb, 1)

                gammab = brow[:, 3, :].unsqueeze(1).broadcast_to([P, J, D])

                def heads(b, t):
                    dve.wait_ge(s_o_ps, nth[b])
                    for k in range(2):
                        last = v.tensor_tensor(t.tmp[:, 1, 4 * k:4 * k + 4, :].rearrange("p j (h e) -> p (j h) e", e=DH),
                                               t.bank[k].rearrange("p (g e) -> p g e", e=DH),
                                               t.rq[:, 4 * k:4 * k + 4, :].rearrange("p j h -> p (j h)").unsqueeze(2)
                                               .broadcast_to([P, 4 * H, DH]), ALU.mult)
                    last.then_inc(s_o_sb, 1)

                def outputs():
                    for b in bs:
                        dve.wait_ge(s_wo_ps, nth[b])
                    lo = batches(bs[0] // PB)[0] * J
                    statistics(lambda j: AT[j // J].tiles(2 + j % J // 4)[:, j % 4, :], lo, PB * J, EPS_ATTN_OUT, s_attn_stats)

                def residual(b, t):
                    dve.wait_ge(s_yn, nth[b])
                    link(v.tensor_tensor(t.tmp[:, 1], t.tmp[:, 1], gammab, ALU.mult))
                    dve.wait_ge(s_beta, nth[b])
                    v.tensor_tensor(xb(b), xb(b), t.tmp[:, 1], ALU.add).then_inc(s_x2, 1)
                    dve.wait_ge(s_x2, nth[b])

                first, second = [(b, AT[b % 2]) for b in bs]
                for b in (first, second):
                    features(*b, 1, s_ek, 2, s_fk)
                features(*first, 0, s_eq, 0, s_fq)
                dots(*first)
                features(*second, 0, s_eq, 0, s_fq)
                states(*first)
                dots(*second)
                states(*second)
                heads(*first)
                heads(*second)
                if bs[0] == 0:
                    combine(2)
                outputs()
                if bs[0] == 0:
                    combine(3)
                residual(*first)
                residual(*second)

            def fold_biases(tile):
                dve.wait_ge(s_brow_in, 16 * 5)
                dve.wait_ge(s_bf_ps, 1)
                v.tensor_tensor(bvcol[:], LB[3][:, 2 * D:2 * D + 1], bcol[:, 3:4], ALU.add)
                link(v.scalar_tensor_tensor(rowrest[:, 0:2, :], LB[3][:, 0:2 * D].rearrange("p (i d) -> p i d", i=2), 1.0,
                                            brow[:, 0:2, :], ALU.add, ALU.add))
                tile()
                link(v.tensor_copy(rowrest[:, 2, :], brow[:, 2, :]))
                for r in (0, 32, 64):
                    link(v.tensor_copy(rowpart[:], rowrest[:]))
                    v.tensor_copy(rows3[r:r + 1], rowpart[r:r + 1])
                    tile()
                    link(v.tensor_tensor(rowrest[:], rowrest[:], rowpart[:], ALU.subtract))
                v.tensor_copy(rows3[64:65], rowpart[64:65]).then_inc(s_bf_sb, 1)

            setup()
            for job in PLAN:
                if job[0] == "N":
                    normal_rows(job[1])
                elif job[0] == "X":
                    turned_rows(job[1])
                elif job[0] == "S":
                    row_statistics(job[1])
                elif job[0] == "T":
                    input_statistics(job[1])
                elif job[0] == "K":
                    choose(job[1])
                elif job[0] == "W":
                    split_weights()
                elif job[0] == "L":
                    low_parts()
                elif job[0] == "C":
                    ffn(job[1])
                elif job[0] == "M":
                    attend(attentions(job[1]))
                elif job[0] == "F":
                    for b in batches(NQ - 1):
                        combine(B + b)


def kernel(**inputs):
    import numpy as _np
    import concourse.bacc as _bacc
    from concourse import mybir as _mybir
    from concourse.bass_utils import run_bass_kernel_spmd as _run

    names = ["L0_attn_" + n for n in ("x", "Wq", "bq", "Wk", "bk", "Wv", "bv", "Wq2", "bq2", "Wk2", "bk2", "Wv2", "bv2",
                                      "Wo", "bo", "gamma", "beta")]
    names += ["L0_ffn_" + n for n in ("gate_w", "w1", "b1", "w2", "b2")]
    nc = _bacc.Bacc("TRN2", target_bir_lowering=False, num_devices=1)
    arrays, args = {}, []
    for name in names:
        a = _np.ascontiguousarray(inputs[name])
        arrays[f"in_{name}_dram"] = a
        args.append(nc.dram_tensor(f"in_{name}_dram", a.shape, _mybir.dt.from_np(a.dtype), kind="ExternalInput").ap())
    args.append(nc.dram_tensor("out_dram", (B, L, D), _mybir.dt.float32, kind="ExternalOutput").ap())
    macaron(nc, *args)
    r = _run(nc, [arrays], core_ids=[0])
    return r.results[0]["out_dram"]
```
